# Optimizing a Trainium2 kernel written in Bass

```python
import numpy as np
import jax
import jax.numpy as jnp

def _softmax(x, axis=-1):
    return jax.nn.softmax(x, axis=axis)

def _gelu(x):
    return jax.nn.gelu(x, approximate=True)

def _silu(x):
    return jax.nn.silu(x)

def _sigmoid(x):
    return jax.nn.sigmoid(x)

def _layernorm(x, axis=-1, eps=1e-05):
    m = jnp.mean(x, axis=axis, keepdims=True)
    v = jnp.var(x, axis=axis, keepdims=True)
    return (x - m) / jnp.sqrt(v + eps)

def _scatter_add(tgt, idx, src, axis=0):
    return tgt.at[idx].add(src)

def _segment_sum(src, seg, n):
    return jax.ops.segment_sum(src, seg, n)
kernel_name = 'mk_decoder_postln_d1_seqx_r4_c02709'

def setup_inputs(seed: int=0):
    np.random.seed(seed)
    _w = jnp.asarray

    def _rec_inputs():
        import jax
        import jax.numpy as jnp
        _rk = jax.random.key(seed)
        x = 7.22e-05 + 1 * jax.random.normal(jax.random.fold_in(_rk, 1), (64, 128, 256), jnp.float32)
        _lenS = 128 - jax.random.randint(jax.random.fold_in(_rk, 7), (64,), 0, max(1, 128 // 4) + 1, jnp.int32)
        _lenS2 = 128 - jax.random.randint(jax.random.fold_in(_rk, 8), (64,), 0, max(1, 128 // 4) + 1, jnp.int32)
        _ctx_1024P = jax.random.normal(jax.random.fold_in(_rk, 11), (64, 16, 256), jnp.float32)
        _ctx_1024c = jax.random.dirichlet(jax.random.fold_in(_rk, 511), 0.3 * jnp.ones((16,), jnp.float32), (64, 128))
        _ctx_1024t = jnp.einsum('bsk,bkd->bsd', _ctx_1024c, _ctx_1024P)
        _ctx_1024t = _ctx_1024t * jax.lax.rsqrt(jnp.mean(jnp.square(_ctx_1024t)) + 1e-12) * 0.953939
        ctx_1024 = 4.13588e-05 + 0.999923 * (_ctx_1024t + 0.3 * jax.random.normal(jax.random.fold_in(_rk, 611), (64, 128, 256), jnp.float32))
        return (x, ctx_1024)
    x, ctx_1024 = _rec_inputs()

    def _L0_attn_setup():
        import jax, jax.numpy as jnp
        import numpy as np
        D_MODEL, D_STATE, D_CONV, EXPAND = (256, 16, 4, 2)
        D_INNER = D_MODEL * EXPAND
        LN_EPS = 1e-05

        def _layernorm(x, gamma, beta):
            mu = jnp.mean(x, axis=-1, keepdims=True)
            var = jnp.mean(jnp.square(x - mu), axis=-1, keepdims=True)
            return (x - mu) * jax.lax.rsqrt(var + LN_EPS) * gamma + beta

        def _selective_scan(x, A, Bmat, Cmat, delta):
            b, l, d = x.shape
            n = A.shape[-1]
            h0 = jnp.zeros((b, d, n), dtype=x.dtype)

            def step(h, inp):
                xt, Bt, Ct, dt = inp
                dA = jnp.exp(dt[:, :, None] * A[None])
                h = dA * h + dt[:, :, None] * Bt[:, None, :] * xt[:, :, None]
                y = jnp.einsum('bdn,bn->bd', h, Ct)
                return (h, y)
            xs = (jnp.swapaxes(x, 0, 1), jnp.swapaxes(Bmat, 0, 1), jnp.swapaxes(Cmat, 0, 1), jnp.swapaxes(delta, 0, 1))
            _, ys = jax.lax.scan(step, h0, xs)
            return jnp.swapaxes(ys, 0, 1)
        key = jax.random.key(seed)
        ks = jax.random.split(key, 8)
        s = 0.02
        x = jax.random.normal(ks[0], (2, 1024, D_MODEL), dtype=jnp.float32)
        W_in = jax.random.normal(ks[1], (D_MODEL, 2 * D_INNER), dtype=jnp.float32) * s
        conv_w = jax.random.normal(ks[2], (D_INNER, 1, D_CONV), dtype=jnp.float32) * 0.3
        conv_b = jax.random.normal(ks[3], (D_INNER,), dtype=jnp.float32) * s
        W_x = jax.random.normal(ks[4], (D_INNER, 2 * D_STATE + 1), dtype=jnp.float32) * s
        A_log = jnp.broadcast_to(jnp.log(jnp.arange(1, D_STATE + 1, dtype=jnp.float32))[None, :], (D_INNER, D_STATE))
        D_skip = jnp.ones((D_INNER,), dtype=jnp.float32)
        W_out = jax.random.normal(ks[5], (D_INNER, D_MODEL), dtype=jnp.float32) * s
        gamma = jnp.ones((D_MODEL,), dtype=jnp.float32)
        beta = jnp.zeros((D_MODEL,), dtype=jnp.float32)
        return {'x': x, 'W_in': W_in, 'conv_w': conv_w, 'conv_b': conv_b, 'W_x': W_x, 'A_log': A_log, 'D_skip': D_skip, 'W_out': W_out, 'gamma': gamma, 'beta': beta}
    _L0_attn_all = _L0_attn_setup()
    _L0_attn_in = {k: v for k, v in _L0_attn_all.items() if k in ('W_in', 'conv_w', 'conv_b', 'W_x', 'A_log', 'D_skip', 'W_out', 'gamma', 'beta')}
    del _L0_attn_all

    def _L0_xattn_setup():
        import jax, jax.numpy as jnp
        import numpy as np
        EMBED_DIM = 256
        HEAD_DIM = 256
        GAMMA = 0.96875
        THETA = 10000.0
        SCALE_BASE = 512.0

        def _dup_interleave(x):
            return jnp.repeat(x, 2, axis=-1)

        def _rotate_half(x):
            x_even = x[..., ::2]
            x_odd = x[..., 1::2]
            return jnp.stack((-x_odd, x_even), axis=-1).reshape(x.shape)

        def _xpos(x, offset=0, inverse_scale=False):
            l = x.shape[-2]
            half = HEAD_DIM // 2
            scale_vec = (jnp.arange(0, HEAD_DIM, 2, dtype=jnp.float32) + 0.4 * HEAD_DIM) / (1.4 * HEAD_DIM)
            pos = jnp.arange(offset, offset + l, dtype=jnp.float32)
            scale = scale_vec[None, :] ** (pos / SCALE_BASE)[:, None]
            freqs = 1.0 / THETA ** (jnp.arange(half, dtype=jnp.float32) / half)
            sin_in = pos[:, None] * freqs[None, :]
            sin, cos = (jnp.sin(sin_in), jnp.cos(sin_in))
            if inverse_scale:
                scale = 1.0 / scale
            return x * _dup_interleave(cos * scale) + _rotate_half(x) * _dup_interleave(sin * scale)

        def _decay_mask(l, gamma):
            idx = jnp.arange(l, dtype=jnp.float32)
            diff = idx[:, None] - idx[None, :]
            return jnp.where(diff >= 0, gamma ** diff, 0.0)
        key = jax.random.key(seed)
        k1, k2, k3, k4, k5, k6 = jax.random.split(key, 6)
        B, L = (4, 512)
        s = 1.0 / np.sqrt(EMBED_DIM)
        return {'q': jax.random.normal(k1, (B, L, EMBED_DIM), dtype=jnp.float32), 'k': jax.random.normal(k2, (B, L, EMBED_DIM), dtype=jnp.float32), 'v': jax.random.normal(k3, (B, L, EMBED_DIM), dtype=jnp.float32), 'Wq': jax.random.normal(k4, (EMBED_DIM, HEAD_DIM), dtype=jnp.float32) * s, 'Wk': jax.random.normal(k5, (EMBED_DIM, HEAD_DIM), dtype=jnp.float32) * s, 'Wv': jax.random.normal(k6, (EMBED_DIM, HEAD_DIM), dtype=jnp.float32) * s}
    _L0_xattn_all = _L0_xattn_setup()
    _L0_xattn_in = {k: v for k, v in _L0_xattn_all.items() if k in ('Wq', 'Wk', 'Wv')}
    del _L0_xattn_all

    def _L0_ffn_setup():
        import jax, jax.numpy as jnp
        import numpy as np
        B, S, H = (2, 512, 256)
        E_ROUTED = 8
        TOP_K = 2
        I = 512
        key = jax.random.key(seed)
        ks = jax.random.split(key, 9)
        s = 0.02
        return {'x': jax.random.normal(ks[0], (B, S, H), dtype=jnp.float32), 'shared_gate': jax.random.normal(ks[1], (I, H), dtype=jnp.float32) * s, 'shared_up': jax.random.normal(ks[2], (I, H), dtype=jnp.float32) * s, 'shared_down': jax.random.normal(ks[3], (H, I), dtype=jnp.float32) * s, 'gate_w': jax.random.normal(ks[4], (E_ROUTED, H, I), dtype=jnp.float32) * s, 'up_w': jax.random.normal(ks[5], (E_ROUTED, H, I), dtype=jnp.float32) * s, 'down_w': jax.random.normal(ks[6], (E_ROUTED, I, H), dtype=jnp.float32) * s, 'router_w': jax.random.normal(ks[7], (E_ROUTED, H), dtype=jnp.float32) * s, 'routing_bias': jnp.zeros((E_ROUTED,), dtype=jnp.float32)}
    _L0_ffn_all = _L0_ffn_setup()
    _L0_ffn_in = {k: v for k, v in _L0_ffn_all.items() if k in ('shared_gate', 'shared_up', 'shared_down', 'gate_w', 'up_w', 'down_w', 'router_w', 'routing_bias')}
    del _L0_ffn_all
    return {'x': x, 'ctx_1024': ctx_1024, 'L0_attn_W_in': _L0_attn_in['W_in'], 'L0_attn_conv_w': _L0_attn_in['conv_w'], 'L0_attn_conv_b': _L0_attn_in['conv_b'], 'L0_attn_W_x': _L0_attn_in['W_x'], 'L0_attn_A_log': _L0_attn_in['A_log'], 'L0_attn_D_skip': _L0_attn_in['D_skip'], 'L0_attn_W_out': _L0_attn_in['W_out'], 'L0_attn_gamma': _L0_attn_in['gamma'], 'L0_attn_beta': _L0_attn_in['beta'], 'L0_xattn_Wq': _L0_xattn_in['Wq'], 'L0_xattn_Wk': _L0_xattn_in['Wk'], 'L0_xattn_Wv': _L0_xattn_in['Wv'], 'L0_ffn_shared_gate': _L0_ffn_in['shared_gate'], 'L0_ffn_shared_up': _L0_ffn_in['shared_up'], 'L0_ffn_shared_down': _L0_ffn_in['shared_down'], 'L0_ffn_gate_w': _L0_ffn_in['gate_w'], 'L0_ffn_up_w': _L0_ffn_in['up_w'], 'L0_ffn_down_w': _L0_ffn_in['down_w'], 'L0_ffn_router_w': _L0_ffn_in['router_w'], 'L0_ffn_routing_bias': _L0_ffn_in['routing_bias']}

def reference(x, ctx_1024, L0_attn_W_in, L0_attn_conv_w, L0_attn_conv_b, L0_attn_W_x, L0_attn_A_log, L0_attn_D_skip, L0_attn_W_out, L0_attn_gamma, L0_attn_beta, L0_xattn_Wq, L0_xattn_Wk, L0_xattn_Wv, L0_ffn_shared_gate, L0_ffn_shared_up, L0_ffn_shared_down, L0_ffn_gate_w, L0_ffn_up_w, L0_ffn_down_w, L0_ffn_router_w, L0_ffn_routing_bias):
    import jax
    import jax.numpy as jnp

    def _L0_attn_ref(x, W_in, conv_w, conv_b, W_x, A_log, D_skip, W_out, gamma, beta):
        import jax, jax.numpy as jnp
        import numpy as np
        D_MODEL, D_STATE, D_CONV, EXPAND = (256, 16, 4, 2)
        D_INNER = D_MODEL * EXPAND
        LN_EPS = 1e-05

        def _layernorm(x, gamma, beta):
            mu = jnp.mean(x, axis=-1, keepdims=True)
            var = jnp.mean(jnp.square(x - mu), axis=-1, keepdims=True)
            return (x - mu) * jax.lax.rsqrt(var + LN_EPS) * gamma + beta

        def _selective_scan(x, A, Bmat, Cmat, delta):
            b, l, d = x.shape
            n = A.shape[-1]
            h0 = jnp.zeros((b, d, n), dtype=x.dtype)

            def step(h, inp):
                xt, Bt, Ct, dt = inp
                dA = jnp.exp(dt[:, :, None] * A[None])
                h = dA * h + dt[:, :, None] * Bt[:, None, :] * xt[:, :, None]
                y = jnp.einsum('bdn,bn->bd', h, Ct)
                return (h, y)
            xs = (jnp.swapaxes(x, 0, 1), jnp.swapaxes(Bmat, 0, 1), jnp.swapaxes(Cmat, 0, 1), jnp.swapaxes(delta, 0, 1))
            _, ys = jax.lax.scan(step, h0, xs)
            return jnp.swapaxes(ys, 0, 1)
        residual = x
        xn = _layernorm(x, gamma, beta)
        xz = xn @ W_in
        x_inner, z = jnp.split(xz, 2, axis=-1)
        xc = jnp.swapaxes(x_inner, 1, 2)
        xc = jax.lax.conv_general_dilated(xc, conv_w, window_strides=(1,), padding=[(D_CONV - 1, 0)], dimension_numbers=('NCH', 'OIH', 'NCH'), feature_group_count=D_INNER)
        xc = xc + conv_b[None, :, None]
        x_conv = jax.nn.silu(jnp.swapaxes(xc, 1, 2))
        xp = x_conv @ W_x
        Bmat = xp[:, :, :D_STATE]
        Cmat = xp[:, :, D_STATE:2 * D_STATE]
        delta = jax.nn.softplus(xp[:, :, -1:])
        A = -jnp.exp(A_log)
        y = _selective_scan(x_conv, A, Bmat, Cmat, delta)
        y = y + x_conv * D_skip[None, None, :]
        y = y * jax.nn.silu(z)
        return y @ W_out + residual

    def _L0_xattn_ref(q, k, v, Wq, Wk, Wv):
        import jax, jax.numpy as jnp
        import numpy as np
        EMBED_DIM = 256
        HEAD_DIM = 256
        GAMMA = 0.96875
        THETA = 10000.0
        SCALE_BASE = 512.0

        def _dup_interleave(x):
            return jnp.repeat(x, 2, axis=-1)

        def _rotate_half(x):
            x_even = x[..., ::2]
            x_odd = x[..., 1::2]
            return jnp.stack((-x_odd, x_even), axis=-1).reshape(x.shape)

        def _xpos(x, offset=0, inverse_scale=False):
            l = x.shape[-2]
            half = HEAD_DIM // 2
            scale_vec = (jnp.arange(0, HEAD_DIM, 2, dtype=jnp.float32) + 0.4 * HEAD_DIM) / (1.4 * HEAD_DIM)
            pos = jnp.arange(offset, offset + l, dtype=jnp.float32)
            scale = scale_vec[None, :] ** (pos / SCALE_BASE)[:, None]
            freqs = 1.0 / THETA ** (jnp.arange(half, dtype=jnp.float32) / half)
            sin_in = pos[:, None] * freqs[None, :]
            sin, cos = (jnp.sin(sin_in), jnp.cos(sin_in))
            if inverse_scale:
                scale = 1.0 / scale
            return x * _dup_interleave(cos * scale) + _rotate_half(x) * _dup_interleave(sin * scale)

        def _decay_mask(l, gamma):
            idx = jnp.arange(l, dtype=jnp.float32)
            diff = idx[:, None] - idx[None, :]
            return jnp.where(diff >= 0, gamma ** diff, 0.0)
        qh = _xpos(q @ Wq, offset=0, inverse_scale=False)
        kh = _xpos(k @ Wk, offset=0, inverse_scale=True)
        vh = v @ Wv
        L = qh.shape[-2]
        mask = _decay_mask(L, GAMMA)
        scores = jnp.einsum('bld,bmd->blm', qh, kh) * mask[None, :, :]
        return scores @ vh

    def _L0_ffn_ref(x, shared_gate, shared_up, shared_down, gate_w, up_w, down_w, router_w, routing_bias):
        import jax, jax.numpy as jnp
        import numpy as np
        B, S, H = (2, 512, 256)
        E_ROUTED = 8
        TOP_K = 2
        I = 512
        b, s, h = x.shape
        shared = jnp.einsum('bsi,hi->bsh', jax.nn.silu(jnp.einsum('bsh,ih->bsi', x, shared_gate)) * jnp.einsum('bsh,ih->bsi', x, shared_up), shared_down)
        logits = jnp.einsum('bsh,eh->bse', x, router_w) + routing_bias
        probs = jax.nn.sigmoid(logits)
        scores, indices = jax.lax.top_k(probs, TOP_K)
        scores = scores / jnp.sum(scores, axis=-1, keepdims=True)
        t = b * s
        xf = x.reshape(t, h)
        idx = indices.reshape(t, TOP_K)
        sc = scores.reshape(t, TOP_K)
        w = jnp.zeros((t, E_ROUTED), dtype=x.dtype)
        w = w.at[jnp.arange(t)[:, None], idx].add(sc)
        g = jax.nn.silu(jnp.einsum('th,ehi->tei', xf, gate_w))
        u = jnp.einsum('th,ehi->tei', xf, up_w)
        combined = jnp.einsum('tei,eih,te->th', g * u, down_w, w)
        return shared + combined.reshape(b, s, h)
    x = _layernorm(x + _L0_attn_ref(x, L0_attn_W_in, L0_attn_conv_w, L0_attn_conv_b, L0_attn_W_x, L0_attn_A_log, L0_attn_D_skip, L0_attn_W_out, L0_attn_gamma, L0_attn_beta), axis=-1)
    x = _layernorm(x + _L0_xattn_ref(x, ctx_1024, ctx_1024, L0_xattn_Wq, L0_xattn_Wk, L0_xattn_Wv), axis=-1)
    x = _layernorm(x + _L0_ffn_ref(x, L0_ffn_shared_gate, L0_ffn_shared_up, L0_ffn_shared_down, L0_ffn_gate_w, L0_ffn_up_w, L0_ffn_down_w, L0_ffn_router_w, L0_ffn_routing_bias), axis=-1)
    return x

_drawn_inputs = setup_inputs


def setup_inputs(seed=0):
    import zlib

    import numpy as np

    out = dict(_drawn_inputs(seed))
    spreads = {'L0_attn_D_skip': (1.0, 0.6),
     'L0_attn_gamma': (1.0, 0.6),
     'L0_attn_beta': (0.0, 0.8),
     'L0_ffn_routing_bias': (0.0, 0.8)}
    factors = {'L0_attn_W_in': 8.0,
     'L0_attn_conv_w': 8.0,
     'L0_attn_conv_b': 8.0,
     'L0_attn_W_x': 8.0,
     'L0_attn_A_log': 8.0,
     'L0_attn_W_out': 8.0,
     'L0_ffn_gate_w': 3.405,
     'L0_ffn_up_w': 3.359,
     'L0_ffn_down_w': 3.362,
     'L0_ffn_router_w': 3.921,
     'L0_ffn_shared_gate': 3.019,
     'L0_ffn_shared_up': 2.991,
     'L0_ffn_shared_down': 2.985}
    for name, (base, spread) in spreads.items():
        noise = np.random.default_rng([zlib.crc32(name.encode()), seed]).standard_normal(out[name].shape)
        drawn = base * np.exp(spread * noise) if base else spread * noise
        out[name] = jnp.asarray(drawn.astype(out[name].dtype))
    for name, factor in factors.items():
        out[name] = (out[name] * factor).astype(out[name].dtype)
    return out
```

```python
from contextlib import ExitStack

import numpy as np

import concourse.bass as bass
from concourse import mybir

F32 = mybir.dt.float32
F32R = mybir.dt.float32r
I32 = mybir.dt.int32
U32 = mybir.dt.uint32
ALU = mybir.AluOpType
ACT = mybir.ActivationFunctionType
AX = mybir.AxisListType

P = 128
SEQS, SEQ_LEN, D_MODEL = 64, 128, 256
D_INNER, D_STATE, D_CONV = 512, 16, 4
EXPERTS, TOP_K, D_FF = 8, 2, 512
TOKENS = SEQS * SEQ_LEN
LN_EPS = 1e-5
GS = 4
GT = GS * SEQ_LEN
GROUPS = SEQS // GS
PAIRS = GROUPS // 2
KM = D_MODEL // P
KI = D_INNER // P
KF = D_FF // P
XP = 2 * D_STATE + 1
SEG = SEQ_LEN + 1
CHUNK = 32
SEG_COLS = P + sum(range(CHUNK, SEQ_LEN, CHUNK))
SLOT_TILES = (TOKENS * TOP_K + EXPERTS * (P - 1)) // P // 2 * 2 + 2
SLOTS = SLOT_TILES * P
ZERO_PARTS = next(n for n in range(16, SLOT_TILES + 1) if SLOT_TILES % n == 0)
ZERO_TILES = SLOT_TILES // ZERO_PARTS

PASSES = [(a, b, k) for k in range(KM) for a, b in ((0, 1), (1, 0), (0, 0))]

GAMMA, THETA, SCALE_BASE = 0.96875, 10000.0, 512.0
CONSTS = ["ident", "upto", "q_cos", "q_sin", "k_cos", "k_sin", "decay", "before"]


def shape_constants():
    f = np.float32
    pos = np.arange(SEQ_LEN, dtype=f)
    half = D_MODEL // 2
    scale_vec = (np.arange(0, D_MODEL, 2, dtype=f) + f(0.4 * D_MODEL)) / f(1.4 * D_MODEL)
    scale = scale_vec[None, :] ** (pos / f(SCALE_BASE))[:, None]
    freqs = f(1.0) / f(THETA) ** (np.arange(half, dtype=f) / f(half))
    angle = pos[:, None] * freqs[None, :]
    sin, cos = np.sin(angle), np.cos(angle)
    row, col = np.arange(P)[:, None], np.arange(P)[None, :]
    diff = (col - row).astype(f)
    decay = np.where(diff >= 0, f(GAMMA) ** np.maximum(diff, 0), 0)
    tables = {
        "ident": row == col, "upto": row <= col, "before": row < col,
        "q_cos": (cos * scale).T, "q_sin": (sin * scale).T,
        "k_cos": (cos * (f(1.0) / scale)).T, "k_sin": (sin * (f(1.0) / scale)).T, "decay": decay,
    }
    return np.ascontiguousarray(np.concatenate([tables[n].astype(f) for n in CONSTS], axis=1))


def chunk_masks():
    k, s = np.arange(SEQ_LEN)[:, None], np.arange(SEQ_LEN)[None, :]
    parts = [(k // CHUNK == s // CHUNK) & (k > s)]
    for end in range(CHUNK, SEQ_LEN, CHUNK):
        parts.append((k >= end) & (k <= s[:, end:]))
    parts.append(k % CHUNK <= s[:, :CHUNK])
    return np.concatenate(parts, axis=1).astype(np.float32)


def routing_tables():
    seq, e, tile = np.arange(SEQS), np.arange(EXPERTS), np.arange(SLOT_TILES)
    parts = (np.broadcast_to(EXPERTS - e, (SEQS, EXPERTS)), np.broadcast_to(P * seq, (EXPERTS, SEQS)),
             np.broadcast_to(tile[:, None], (SLOT_TILES, EXPERTS)))
    return np.concatenate([a.astype(np.float32).ravel() for a in parts])


def const_cols(name):
    i = CONSTS.index(name)
    return slice(i * P, (i + 1) * P)


def allocators(nc, ctx, stage):
    return (lambda name, *a: ctx.enter_context(nc.sbuf_tensor(f"{stage}_{name}", *a)),
            lambda name, *a: ctx.enter_context(nc.psum_tensor(f"{stage}_{name}", *a)),
            lambda name: ctx.enter_context(nc.semaphore(f"{stage}_{name}")))


def clear_semaphores(nc):
    ids = sorted(nc.released_uncleared_semaphores)
    starts = [i for i in ids if i - 1 not in ids]
    ends = [i + 1 for i in ids if i + 1 not in ids]
    with nc.Block() as block:

        @block.vector
        def _(dve):
            for start, end in zip(starts, ends):
                dve.sem_clear(range(start, end))


def in_pairs(eng, body, count=PAIRS):
    body(0, False)
    with eng.Fori(1, count - 1) as pair:
        body(pair, False)
    body(count - 1, True)


def mamba_in(nc, d):
    with ExitStack() as ctx:
        sb, ps, sem = allocators(nc, ctx, "mamba_in")
        w_in = sb("w_in", [P, KM, 2 * D_INNER], F32)
        w_x = sb("w_x", [P, KI, XP], F32)
        ident = sb("ident", [P, P], F32)
        gamma_beta = sb("gamma_beta", [P, 2, KM], F32)
        conv_wb = sb("conv_wb", [P, KI, D_CONV + 1], F32)
        neg_half = sb("neg_half", [P, GS], F32)
        x_rows = sb("x_rows", [P, 2, GS, D_MODEL], F32)
        x_norm = sb("x_norm", [P, 2, GS, D_MODEL], F32)
        stats = sb("stats", [P, 2, GS, 6], F32)
        mean_var = sb("mean_var", [P, 2, GS, 2], F32)
        rstd = sb("rstd", [P, 2, GS], F32)
        w_in_parts = sb("w_in_parts", [P, 2, KM, 2 * D_INNER], F32R)
        affine = sb("affine", [P, KM, GT], F32)
        xn_T = sb("xn_T", [P, 2, 2, KM, GT], F32R)
        conv = sb("conv", [P, 2, KI, GT], F32)
        xc_T = sb("xc_T", [P, 2, KI, GT], F32)
        gate_T = sb("gate_T", [P, 2, KI, GT], F32)
        xp_T = sb("xp_T", [XP, 2, GT], F32)
        ps_turn = ps("ps_turn", [P, KM, GT], F32)
        ps_inner = ps("ps_inner", [P, 2, GT], F32)
        ps_gate = ps("ps_gate", [P, 2, GT], F32)
        ps_xp = ps("ps_xp", [P, GT], F32)
        weights_loaded = sem("weights_loaded")
        x_loaded = [sem(f"x_loaded_{u}") for u in range(2)]
        const_ready = sem("const_ready")
        stats_ready = sem("stats_ready")
        mean_ready = sem("mean_ready")
        var_eps_ready = sem("var_eps_ready")
        rstd_ready = sem("rstd_ready")
        norm_ready = sem("norm_ready")
        turned = sem("turned")
        affine_ready = sem("affine_ready")
        high_ready = sem("high_ready")
        w_in_ready = sem("w_in_ready")
        xn_T_ready = sem("xn_T_ready")
        inner_done = sem("inner_done")
        gate_done = sem("gate_done")
        gate_T_ready = sem("gate_T_ready")
        tap_done = sem("tap_done")
        bias_tap_done = sem("bias_tap_done")
        xc_ready = sem("xc_ready")
        xp_done = sem("xp_done")
        xp_T_ready = sem("xp_T_ready")
        xc_stored = [sem(f"xc_stored_{u}") for u in range(2)]
        gate_stored = [sem(f"gate_stored_{u}") for u in range(2)]
        xp_stored = [sem(f"xp_stored_{u}") for u in range(2)]
        dve_passed = sem("dve_passed")
        pool_passed = sem("pool_passed")
        block = ctx.enter_context(nc.Block())
        AHEAD_AT = KI - 2
        TAPS = D_CONV - 1

        @block.sync
        def _(sp):
            for stored in (*gate_stored, *xc_stored, *xp_stored):
                sp.sem_inc(stored, 16)
            sp.dma_start(ident[:], d["consts"][:, const_cols("ident")]).then_inc(weights_loaded, 16)
            sp.dma_start(x_rows[:, 0], d["x"][0]).then_inc(x_loaded[0], 16)
            sp.dma_start(w_in[:], d["W_in"]).then_inc(weights_loaded, 16)
            sp.dma_start(gamma_beta[:, 0], d["gamma"]).then_inc(weights_loaded, 16)
            sp.dma_start(gamma_beta[:, 1], d["beta"]).then_inc(weights_loaded, 16)
            sp.dma_start(conv_wb[:], d["conv_wb"]).then_inc(weights_loaded, 16)
            sp.dma_start(w_x[:], d["W_x"]).then_inc(weights_loaded, 16)
            sp.dma_start(x_rows[:, 1], d["x"][1]).then_inc(x_loaded[1], 16)

            def body(pair, last):
                for u in range(2):
                    g = 2 * pair + u
                    if not last:
                        sp.wait_ge(norm_ready, GS * (g + 1))
                        sp.dma_start(x_rows[:, u], d["x"][g + 2]).then_inc(x_loaded[u], 16)
                    sp.wait_ge(gate_T_ready, KI * (g + 1) + 2)
                    sp.dma_start(d["gate_T"][g], gate_T[:, u]).then_inc(gate_stored[u], 16)
                    sp.wait_ge(xc_ready, KI * (g + 1))
                    sp.dma_start(d["xc_T"][g], xc_T[:, u]).then_inc(xc_stored[u], 16)
                    sp.wait_ge(xp_T_ready, g + 1)
                    sp.dma_start(d["xp_T"][g], xp_T[:, u]).then_inc(xp_stored[u], 16)

            in_pairs(sp, body)
            for stored in (*gate_stored, *xc_stored, *xp_stored):
                sp.wait_ge(stored, 16 * (PAIRS + 1))

        @block.gpsimd
        def _(pool):
            nc.gpsimd.memset(neg_half[:], -0.5).then_inc(const_ready, 1)
            pool.wait_ge(const_ready, 1)
            with pool.Fori(0, PAIRS) as pair:
                for u in range(2):
                    g = 2 * pair + u
                    pool.wait_ge(mean_ready, GS * (g + 1))
                    pool.sem_inc(pool_passed, 1)
                    nc.gpsimd.tensor_scalar(rstd[:, u], mean_var[:, u, :, 1], LN_EPS, None,
                                            ALU.add).then_inc(var_eps_ready, 1)
                    pool.wait_ge(var_eps_ready, g + 1)
                    nc.gpsimd.tensor_tensor(rstd[:, u], rstd[:, u], neg_half[:], ALU.pow).then_inc(rstd_ready, 1)

        @block.vector
        def _(dve):
            dve.sem_inc(tap_done, 2 * TAPS)
            dve.wait_ge(weights_loaded, 6 * 16)

            def statistics(g, u, nth):
                dve.wait_ge(x_loaded[u], 16 * nth)
                for s in range(GS):
                    nc.vector.bn_stats(stats[:, u, s], x_rows[:, u, s]).then_inc(stats_ready, 1)
                dve.wait_ge(stats_ready, GS * (g + 1))
                dve.sem_inc(dve_passed, 1)
                for s in range(GS):
                    nc.vector.bn_aggr(mean_var[:, u, s], stats[:, u, s]).then_inc(mean_ready, 1)

            def normalise(g, u):
                dve.wait_ge(rstd_ready, g + 1)
                dve.wait_ge(mean_ready, GS * (g + 1))
                for s in range(GS):
                    nc.vector.tensor_scalar(x_norm[:, u, s], x_rows[:, u, s], mean_var[:, u, s, 0:1],
                                            rstd[:, u, s:s + 1], ALU.subtract, ALU.mult).then_inc(norm_ready, 1)

            def convolve(g, u, j):
                dve.wait_ge(bias_tap_done, KI * g + j + 1)
                out = conv[:, u, j].rearrange("p (s t) -> p s t", s=GS)
                now = ps_inner[:, j % 2].rearrange("p (s t) -> p s t", s=GS)
                for lag in range(1, D_CONV):
                    if lag > 1:
                        dve.wait_ge(tap_done, TAPS * (2 + KI * g + j) + lag - 1)
                    op = nc.vector.scalar_tensor_tensor(
                        out[:, :, lag:], now[:, :, :SEQ_LEN - lag], conv_wb[:, j, D_CONV - 1 - lag:D_CONV - lag],
                        out[:, :, lag:], ALU.mult, ALU.add)
                    op.then_inc(tap_done, 1)

            def split(g, u):
                for k in range(KM):
                    dve.wait_ge(affine_ready, KM * g + k + 1)
                    nc.vector.tensor_copy(xn_T[:, u, 0, k], affine[:, k]).then_inc(high_ready, 1)
                for k in range(KM):
                    dve.wait_ge(high_ready, KM * g + k + 1)
                    nc.vector.tensor_tensor(xn_T[:, u, 1, k], affine[:, k], xn_T[:, u, 0, k].bitcast(F32),
                                            ALU.subtract).then_inc(xn_T_ready, 1)

            statistics(0, 0, 1)
            normalise(0, 0)
            nc.vector.tensor_copy(w_in_parts[:, 0], w_in[:]).then_inc(w_in_ready, 1)
            dve.wait_ge(w_in_ready, 1)
            nc.vector.tensor_tensor(w_in_parts[:, 1], w_in[:], w_in_parts[:, 0].bitcast(F32),
                                    ALU.subtract).then_inc(w_in_ready, 1)
            split(0, 0)

            def body(pair, last):
                for u in range(2):
                    g = 2 * pair + u
                    ahead = not (last and u)
                    if ahead:
                        statistics(g + 1, 1 - u, pair + 1 + u)
                    convolve(g, u, 0)
                    if ahead:
                        dve.wait_ge(turned, g)
                        normalise(g + 1, 1 - u)
                    for j in range(1, KI):
                        convolve(g, u, j)
                        if j == AHEAD_AT and ahead:
                            split(g + 1, 1 - u)

            in_pairs(dve, body)

        @block.scalar
        def _(act):
            act.wait_ge(weights_loaded, 6 * 16)
            act.sem_inc(gate_T_ready, 2)

            def evacuate_turned(g):
                for k in range(KM):
                    act.wait_ge(turned, g + 1)
                    nc.scalar.activation(affine[:, k], ps_turn[:, k], ACT.Identity, scale=gamma_beta[:, 0, k:k + 1],
                                         bias=gamma_beta[:, 1, k:k + 1]).then_inc(affine_ready, 1)

            def bias_tap(g, u, j):
                act.wait_ge(inner_done, KI * g + j + 1)
                nc.scalar.activation(conv[:, u, j], ps_inner[:, j % 2], ACT.Identity,
                                     scale=conv_wb[:, j, D_CONV - 1:D_CONV],
                                     bias=conv_wb[:, j, D_CONV:D_CONV + 1]).then_inc(bias_tap_done, 1)

            def gate(g, u, j):
                act.wait_ge(gate_done, KI * g + j + 1)
                nc.scalar.activation(gate_T[:, u, j], ps_gate[:, j % 2], ACT.Silu).then_inc(gate_T_ready, 1)

            def silu_conv(g, u, j):
                act.wait_ge(tap_done, TAPS * (2 + KI * g + j + 1))
                nc.scalar.activation(xc_T[:, u, j], conv[:, u, j], ACT.Silu).then_inc(xc_ready, 1)

            evacuate_turned(0)

            def body(pair, last):
                for u in range(2):
                    g = 2 * pair + u
                    act.wait_ge(gate_stored[u], 16 * (pair + 1))
                    act.wait_ge(xc_stored[u], 16 * (pair + 1))
                    for j in range(KI):
                        bias_tap(g, u, j)
                        gate(g, u, j)
                        if j:
                            silu_conv(g, u, j - 1)
                        if j == AHEAD_AT and not (last and u):
                            evacuate_turned(g + 1)
                    silu_conv(g, u, KI - 1)
                    act.wait_ge(xp_stored[u], 16 * (pair + 1))
                    act.wait_ge(xp_done, g + 1)
                    nc.scalar.activation(xp_T[:, u], ps_xp[0:XP, :], ACT.Copy).then_inc(xp_T_ready, 1)

            in_pairs(act, body)

        @block.tensor
        def _(pe):
            pe.wait_ge(weights_loaded, 6 * 16)

            def turn(g, u):
                pe.wait_ge(norm_ready, GS * (g + 1))
                pe.wait_ge(affine_ready, KM * g)
                for k in range(KM):
                    for s in range(GS):
                        op = nc.tensor.transpose(ps_turn[:, k, s * P:(s + 1) * P],
                                                 x_norm[:, u, s, k * P:(k + 1) * P], ident[:])
                op.then_inc(turned, 1)

            turn(0, 0)
            pe.wait_ge(w_in_ready, 2)

            def body(pair, last):
                for u in range(2):
                    g = 2 * pair + u
                    pe.wait_ge(xn_T_ready, KM * (g + 1))
                    for j in range(KI):
                        for first, ps, free, per, done in ((j, ps_inner, tap_done, TAPS, inner_done),
                                                           (KI + j, ps_gate, gate_T_ready, 1, gate_done)):
                            pe.wait_ge(free, per * (KI * g + j + 1))
                            for n, (w_part, x_part, k) in enumerate(PASSES):
                                op = nc.tensor.matmul(ps[:, j % 2], w_in_parts[:, w_part, k, first * P:(first + 1) * P],
                                                      xn_T[:, u, x_part, k], start=(n == 0), stop=(n == len(PASSES) - 1))
                            op.then_inc(done, 1)
                        if j == AHEAD_AT and not (last and u):
                            turn(g + 1, 1 - u)
                    pe.wait_ge(xp_T_ready, g)
                    for j in range(KI):
                        pe.wait_ge(xc_ready, KI * g + j + 1)
                        op = nc.tensor.matmul(ps_xp[0:XP, :], w_x[:, j], xc_T[:, u, j], start=(j == 0),
                                              stop=(j == KI - 1))
                    op.then_inc(xp_done, 1)

            in_pairs(pe, body)


def step_sizes(nc, d):
    COLS = TOKENS // P
    TERMS = 9
    with ExitStack() as ctx:
        sb, ps, sem = allocators(nc, ctx, "step_sizes")
        dt = sb("dt", [P, COLS], F32)
        u = sb("u", [P, COLS], F32)
        r = sb("r", [P, COLS], F32)
        r2 = sb("r2", [P, COLS], F32)
        series = sb("series", [P, COLS], F32)
        moved = sem("moved")
        negated = sem("negated")
        exp_ready = sem("exp_ready")
        step = sem("step")
        block = ctx.enter_context(nc.Block())
        STEPS = 5 + TERMS + 2

        @block.sync
        def _(sp):
            sp.dma_start(dt[:], d["dt_row"].rearrange("(p c) -> p c", p=P)).then_inc(moved, 16)
            sp.wait_ge(step, STEPS)
            sp.dma_start(d["delta"].rearrange("(p c) -> p c", p=P), series[:]).then_inc(moved, 16)
            sp.wait_ge(moved, 32)

        @block.scalar
        def _(act):
            act.wait_ge(moved, 16)
            nc.scalar.activation(r[:], dt[:], ACT.Abs).then_inc(negated, 1)
            act.wait_ge(negated, 1)
            nc.scalar.activation(u[:], r[:], ACT.Exp, scale=-1.0).then_inc(exp_ready, 1)

        @block.vector
        def _(dve):
            done = 0

            def then(op):
                nonlocal done
                op.then_inc(step, 1)
                done += 1
                dve.wait_ge(step, done)

            dve.wait_ge(exp_ready, 1)
            then(nc.vector.tensor_scalar(r2[:], u[:], 2.0, None, ALU.add))
            then(nc.vector.reciprocal(r2[:], r2[:]))
            then(nc.vector.tensor_tensor(r[:], u[:], r2[:], ALU.mult))
            then(nc.vector.tensor_tensor(r2[:], r[:], r[:], ALU.mult))
            then(nc.vector.tensor_scalar(series[:], r2[:], 1.0 / (2 * TERMS + 1), None, ALU.mult))
            for k in range(TERMS - 1, 0, -1):
                then(nc.vector.scalar_tensor_tensor(series[:], series[:], 1.0 / (2 * k + 1), r2[:], ALU.add, ALU.mult))
            then(nc.vector.scalar_tensor_tensor(series[:], series[:], 1.0, r[:], ALU.add, ALU.mult))
            then(nc.vector.tensor_scalar(dt[:], dt[:], 0.0, None, ALU.max))
            then(nc.vector.scalar_tensor_tensor(series[:], series[:], 2.0, dt[:], ALU.mult, ALU.add))
            assert done == STEPS


def mamba_scan(nc, d, same_rows):
    RING = 4
    PART = 4
    N = D_STATE
    with ExitStack() as ctx:
        sb, ps, sem = allocators(nc, ctx, "mamba_scan")
        w_out = sb("w_out", [P, KI, D_MODEL], F32)
        ident = sb("ident", [P, P], F32)
        a_log = sb("a_log", [P, KI, N], F32)
        a_neg = sb("a_neg", [P, KI, N], F32)
        d_skip = sb("d_skip", [P, KI], F32)
        neg_half = sb("neg_half", [P, GS], F32)
        delta = sb("delta", [P, 2, GT], F32)
        b_bc = sb("b_bc", [P, N, GT], F32)
        c_bc = sb("c_bc", [P, N, GT], F32)
        xc_T = sb("xc_T", [P, 2, KI, GT], F32)
        gate_T = sb("gate_T", [P, KI, GT], F32)
        x_rows = sb("x_rows", [P, GS, D_MODEL], F32)
        dx = sb("dx", [P, 2, GT], F32)
        dA = sb("dA", [P, RING, GS, SEG], F32)
        dBx = sb("dBx", [P, RING, GS, SEG], F32)
        h = sb("h", [P, RING, GS, SEG], F32)
        hC = sb("hC", [P, RING, GT], F32)
        y_T = sb("y_T", [P, KI, GT], F32)
        sum_rows = sb("sum_rows", [P, GS, D_MODEL], F32)
        x1 = sb("x1", [P, GS, D_MODEL], F32)
        stats = sb("stats", [P, GS, 6], F32)
        mean_var = sb("mean_var", [P, GS, 2], F32)
        rstd = sb("rstd", [P, GS], F32)
        ps_y = ps("ps_y", [P, 2, GT], F32)
        ps_out = ps("ps_out", [P, GS, D_MODEL], F32)
        weights_loaded = sem("weights_loaded")
        a_ready = sem("a_ready")
        zeroed = sem("zeroed")
        b_loaded = [sem(f"b_loaded_{m}") for m in range(N // PART)]
        c_loaded = [sem(f"c_loaded_{m}") for m in range(N // PART)]
        delta_loaded = [sem(f"delta_loaded_{u}") for u in range(2)]
        xc_loaded = [sem(f"xc_loaded_{u}") for u in range(2)]
        gate_loaded = sem("gate_loaded")
        x_loaded = sem("x_loaded")
        dx_ready = sem("dx_ready")
        dA_ready = sem("dA_ready")
        dBx_ready = sem("dBx_ready")
        h_ready = sem("h_ready")
        hC_ready = sem("hC_ready")
        accumulated = sem("accumulated")
        skip_added = sem("skip_added")
        y_ready = sem("y_ready")
        out_done = sem("out_done")
        sum_ready = sem("sum_ready")
        stats_ready = sem("stats_ready")
        mean_ready = sem("mean_ready")
        var_eps_ready = sem("var_eps_ready")
        rstd_ready = sem("rstd_ready")
        norm_ready = sem("norm_ready")
        stored = sem("stored")
        dve_passed = sem("dve_passed")
        pool_passed = sem("pool_passed")
        block = ctx.enter_context(nc.Block())
        STEPS = KI * N

        @block.sync
        def _(sp):
            same = sp.value_load(same_rows[0:1, 0:1], min_val=0, max_val=1)
            with sp.If(same == 0):
                for dst, src in ((a_log, d["A_log"]), (d_skip, d["D_skip"]), (ident, d["consts"][:, const_cols("ident")]),
                                 (w_out, d["W_out"])):
                    sp.dma_start(dst[:], src).then_inc(weights_loaded, 16)

                def body(pair, last):
                    for u in range(2):
                        g = 2 * pair + u
                        sp.wait_ge(y_ready, KI * g)
                        sp.dma_start(delta[:, u], d["delta_groups"][g].partition_broadcast(P)).then_inc(delta_loaded[u], 16)
                        sp.dma_start(xc_T[:, u], d["xc_T"][g]).then_inc(xc_loaded[u], 16)
                        for m in range(N // PART):
                            rows = slice(m * PART, (m + 1) * PART)
                            sp.wait_ge(hC_ready, STEPS * g + (m + 1) * PART)
                            for dst, first, loaded in ((b_bc, 0, b_loaded), (c_bc, N, c_loaded)):
                                sp.dma_start(dst[:, rows], d["xp_rows"][first + m * PART:first + (m + 1) * PART, g]
                                             .partition_broadcast(P)).then_inc(loaded[m], 16)
                        sp.wait_ge(y_ready, KI * (g + 1))
                        sp.dma_start(gate_T[:], d["gate_T"][g]).then_inc(gate_loaded, 16)
                        sp.wait_ge(sum_ready, 2 * g)
                        sp.dma_start(x_rows[:], d["x"][g]).then_inc(x_loaded, 16)

                in_pairs(sp, body)
                sp.wait_ge(stored, 16 * GROUPS)

        def by_seq(row):
            return row.rearrange("p (s t) -> p s t", s=GS)

        @block.gpsimd
        def _(pool):
            same = pool.value_load(same_rows[0:1, 0:1], min_val=0, max_val=1)
            with pool.If(same == 0):
                nc.gpsimd.memset(neg_half[:], -0.5).then_inc(zeroed, 1)
                nc.gpsimd.memset(dA[:, :, :, 0:1], 0.0).then_inc(zeroed, 1)
                nc.gpsimd.memset(dBx[:, :, :, 0:1], 0.0).then_inc(zeroed, 1)
                pool.wait_ge(zeroed, 3)

                def body(pair, last):
                    for u in range(2):
                        g = 2 * pair + u
                        for j in range(KI):
                            pool.wait_ge(dx_ready, KI * g + j + 1)
                            for n in range(N):
                                i = j * N + n
                                if i < N and n % PART == 0:
                                    pool.wait_ge(b_loaded[n // PART], 16 * (g + 1))
                                pool.wait_ge(h_ready, STEPS * g + i + 1)
                                nc.gpsimd.tensor_tensor(dBx[:, i % RING, :, 1:], by_seq(dx[:, j % 2]), by_seq(b_bc[:, n]),
                                                        ALU.mult).then_inc(dBx_ready, 1)
                        pool.wait_ge(mean_ready, GS * (g + 1))
                        pool.sem_inc(pool_passed, 1)
                        nc.gpsimd.tensor_scalar(rstd[:], mean_var[:, :, 1], LN_EPS, None,
                                                ALU.add).then_inc(var_eps_ready, 1)
                        pool.wait_ge(var_eps_ready, g + 1)
                        nc.gpsimd.tensor_tensor(rstd[:], rstd[:], neg_half[:], ALU.pow).then_inc(rstd_ready, 1)
                        pool.wait_ge(norm_ready, GS * (g + 1))
                        pool.dma_start(d["x1"][g], x1[:]).then_inc(stored, 16)

                in_pairs(pool, body)

        @block.scalar
        def _(act):
            same = act.value_load(same_rows[0:1, 0:1], min_val=0, max_val=1)
            with act.If(same == 0):
                act.wait_ge(weights_loaded, 64)
                nc.scalar.activation(a_neg[:], a_log[:], ACT.Exp).then_inc(a_ready, 1)
                act.wait_ge(a_ready, 1)
                nc.scalar.activation(a_neg[:], a_neg[:], ACT.Copy, scale=-1.0).then_inc(a_ready, 1)
                act.wait_ge(a_ready, 2)
                act.wait_ge(zeroed, 3)

                def body(pair, last):
                    for u in range(2):
                        g = 2 * pair + u
                        act.wait_ge(delta_loaded[u], 16 * (pair + 1))
                        for i in range(STEPS):
                            j, n = divmod(i, N)
                            act.wait_ge(h_ready, STEPS * g + i + 1)
                            nc.scalar.activation(dA[:, i % RING, :, 1:], by_seq(delta[:, u]), ACT.Exp,
                                                 scale=a_neg[:, j, n:n + 1]).then_inc(dA_ready, 1)

                in_pairs(act, body)

        @block.vector
        def _(dve):
            same = dve.value_load(same_rows[0:1, 0:1], min_val=0, max_val=1)
            with dve.If(same == 0):
                dve.sem_inc(h_ready, RING)
                dve.sem_inc(hC_ready, N)
                dve.sem_inc(y_ready, KI)
                dve.wait_ge(weights_loaded, 64)

                def step_input(g, u, j, nth):
                    if j == 0:
                        dve.wait_ge(delta_loaded[u], 16 * nth)
                        dve.wait_ge(xc_loaded[u], 16 * nth)
                    dve.wait_ge(dBx_ready, STEPS * g + max(j - 1, 0) * N)
                    nc.vector.tensor_tensor(dx[:, j % 2], delta[:, u], xc_T[:, u, j], ALU.mult).then_inc(dx_ready, 1)

                def scan(g, i):
                    dve.wait_ge(dA_ready, STEPS * g + i + 1)
                    dve.wait_ge(dBx_ready, STEPS * g + i + 1)
                    b = i % RING
                    nc.vector.tensor_tensor_scan(h[:, b].rearrange("p s t -> p (s t)"),
                                                 dA[:, b].rearrange("p s t -> p (s t)"),
                                                 dBx[:, b].rearrange("p s t -> p (s t)"), 0.0, ALU.mult,
                                                 ALU.add).then_inc(h_ready, 1)

                def times_c(g, i):
                    n = i % N
                    if i < N and n % PART == 0:
                        dve.wait_ge(c_loaded[n // PART], 16 * (g + 1))
                    dve.wait_ge(h_ready, RING + STEPS * g + i + 1)
                    dve.wait_ge(accumulated, STEPS * g + i + 1)
                    nc.vector.tensor_tensor(by_seq(hC[:, i % RING]), h[:, i % RING, :, 1:], by_seq(c_bc[:, n]),
                                            ALU.mult).then_inc(hC_ready, 1)

                def finish_chunk(g, u, j):
                    dve.wait_ge(accumulated, RING + STEPS * g + (j + 1) * N)
                    dve.wait_ge(out_done, g)
                    nc.vector.scalar_tensor_tensor(y_T[:, j], xc_T[:, u, j], d_skip[:, j:j + 1], ps_y[:, j % 2], ALU.mult,
                                                   ALU.add).then_inc(skip_added, 1)
                    if j == 0:
                        dve.wait_ge(gate_loaded, 16 * (g + 1))
                    dve.wait_ge(skip_added, KI * g + j + 1)
                    nc.vector.tensor_tensor(y_T[:, j], y_T[:, j], gate_T[:, j], ALU.mult).then_inc(y_ready, 1)

                def body(pair, last):
                    for u in range(2):
                        g = 2 * pair + u
                        step_input(g, u, 0, pair + 1)
                        for i in range(STEPS):
                            scan(g, i)
                            if i:
                                times_c(g, i - 1)
                            if i % N == 4 and i > N:
                                finish_chunk(g, u, i // N - 1)
                            if i % N == N - 2 and i // N + 1 < KI:
                                step_input(g, u, i // N + 1, pair + 1)
                        times_c(g, STEPS - 1)
                        finish_chunk(g, u, KI - 1)
                        dve.wait_ge(out_done, g + 1)
                        dve.wait_ge(x_loaded, 16 * (g + 1))
                        for s in range(0, GS, 2):
                            nc.vector.scalar_tensor_tensor(sum_rows[:, s:s + 2], x_rows[:, s:s + 2], 2.0, ps_out[:, s:s + 2],
                                                           ALU.mult, ALU.add).then_inc(sum_ready, 1)
                        for s in range(GS):
                            dve.wait_ge(sum_ready, 2 * g + s // 2 + 1)
                            nc.vector.bn_stats(stats[:, s], sum_rows[:, s]).then_inc(stats_ready, 1)
                        dve.wait_ge(stats_ready, GS * (g + 1))
                        dve.sem_inc(dve_passed, 1)
                        for s in range(GS):
                            nc.vector.bn_aggr(mean_var[:, s], stats[:, s]).then_inc(mean_ready, 1)
                        dve.wait_ge(rstd_ready, g + 1)
                        dve.wait_ge(mean_ready, GS * (g + 1))
                        dve.wait_ge(stored, 16 * g)
                        for s in range(GS):
                            nc.vector.tensor_scalar(x1[:, s], sum_rows[:, s], mean_var[:, s, 0:1], rstd[:, s:s + 1],
                                                    ALU.subtract, ALU.mult).then_inc(norm_ready, 1)

                in_pairs(dve, body)

        @block.tensor
        def _(pe):
            same = pe.value_load(same_rows[0:1, 0:1], min_val=0, max_val=1)
            with pe.If(same == 0):
                pe.wait_ge(weights_loaded, 64)
                pe.sem_inc(accumulated, RING)

                def body(pair, last):
                    for u in range(2):
                        g = 2 * pair + u
                        for i in range(STEPS):
                            j, n = divmod(i, N)
                            if n == 0:
                                pe.wait_ge(y_ready, KI * (g + 1) + max(j - 1, 0))
                            pe.wait_ge(hC_ready, N + STEPS * g + i + 1)
                            nc.tensor.matmul(ps_y[:, j % 2], ident[:], hC[:, i % RING], start=(n == 0),
                                             stop=(n == N - 1)).then_inc(accumulated, 1)
                        pe.wait_ge(sum_ready, 2 * g)
                        pe.wait_ge(y_ready, KI * (g + 2))
                        for s in range(GS):
                            for j in range(KI):
                                op = nc.tensor.matmul(ps_out[:, s], y_T[:, j, s * P:(s + 1) * P], w_out[:, j],
                                                      start=(j == 0), stop=(j == KI - 1))
                        op.then_inc(out_done, 1)

                in_pairs(pe, body)



def scan_choice(nc, d, same_rows):
    with ExitStack() as ctx:
        sb, ps, sem = allocators(nc, ctx, "scan_choice")
        a_log = sb("a_log", [P, KI, D_STATE], F32)
        row = sb("row", [P, KI, D_STATE], F32)
        equal = sb("equal", [P, KI, D_STATE], F32)
        least = sb("least", [P, 1], F32)
        ones = sb("ones", [P, 1], F32)
        flag = sb("flag", [1, 1], F32)
        ps_count = ps("ps_count", [1, 1], F32)
        loaded = sem("loaded")
        step = sem("step")
        counted = sem("counted")
        block = ctx.enter_context(nc.Block())

        @block.sync
        def _(sp):
            sp.dma_start(a_log[:], d["A_log"]).then_inc(loaded, 16)
            for j in range(KI):
                sp.dma_start(row[:, j], d["A_log"][0, 0].partition_broadcast(P)).then_inc(loaded, 16)
            sp.wait_ge(loaded, 16 * (KI + 1))

        @block.vector
        def _(dve):
            nc.vector.memset(ones[:], 1.0).then_inc(step, 1)
            dve.wait_ge(loaded, 16 * (KI + 1))
            nc.vector.tensor_tensor(equal[:], a_log[:], row[:], ALU.is_equal).then_inc(step, 1)
            dve.wait_ge(step, 2)
            nc.vector.tensor_reduce(least[:], equal[:], AX.XY, ALU.min).then_inc(step, 1)
            dve.wait_ge(counted, 1)
            nc.vector.tensor_scalar(flag[:], ps_count[:], float(P), None, ALU.is_equal).then_inc(step, 1)
            dve.wait_ge(step, 4)
            nc.vector.tensor_copy(same_rows[:], flag[:]).then_inc(step, 1)

        @block.tensor
        def _(pe):
            pe.wait_ge(step, 3)
            nc.tensor.matmul(ps_count[:], least[:], ones[:], start=True, stop=True).then_inc(counted, 1)


def chunk_products(nc, d, same_rows, products):
    C, N = CHUNK, D_STATE
    LATER = [(c, SEQ_LEN - (c + 1) * C) for c in range(SEQ_LEN // C - 1)]
    PARTS = 1 + len(LATER)
    with ExitStack() as ctx:
        sb, ps, sem = allocators(nc, ctx, "chunk_products")
        ident = sb("ident", [P, P], F32)
        masks = sb("masks", [P, SEG_COLS + C], F32)
        delta_rows = sb("delta_rows", [SEQS, SEQ_LEN], F32)
        delta_T = sb("delta_T", [P, SEQS], F32)
        a_bc = sb("a_bc", [P, N], F32)
        a_col = sb("a_col", [N, 1], F32)
        bc_rows = sb("bc_rows", [2 * N, 2, GT], F32)
        c_rows = sb("c_rows", [N, 2, GT], F32)
        step_masks = sb("step_masks", [P, 2, GS, P], F32)
        step_wide = sb("step_wide", [P, 2, GS, N], F32)
        seg_bc = sb("seg_bc", [P, 2, 2, GS, C], F32)
        c_turned = sb("c_turned", [P, 2, GS, N, C], F32)
        decay = sb("decay", [P, 2, GS, N, C], F32)
        inside = sb("inside", [P, GS, C], F32)
        row_decay = sb("row_decay", [N, 2, GS, SEG_COLS], F32)
        row_parts = sb("row_parts", [N, 2, GS, SEG_COLS], F32)
        ps_seg = ps("ps_seg", [P, 2, 512], F32)
        ps_rows = ps("ps_rows", [P, 2, 512], F32)
        ps_off = ps("ps_off", [P, 2, 512], F32)
        ps_delta = ps("ps_delta", [P, 512], F32)
        loaded = sem("loaded")
        a_ready = sem("a_ready")
        cleared = sem("cleared")
        rows_loaded = [sem(f"rows_loaded_{u}") for u in range(2)]
        delta_turned = sem("delta_turned")
        delta_ready = sem("delta_ready")
        steps_ready = sem("steps_ready")
        seg_done = sem("seg_done")
        seg_ready = sem("seg_ready")
        rows_done = sem("rows_done")
        row_decay_ready = sem("row_decay_ready")
        row_parts_ready = sem("row_parts_ready")
        c_turned_ready = sem("c_turned_ready")
        bc_ready = sem("bc_ready")
        decay_ready = sem("decay_ready")
        weighted = sem("weighted")
        inside_ready = sem("inside_ready")
        off_done = sem("off_done")
        off_ready = sem("off_ready")
        pe_passed = sem("pe_passed")
        dve_passed = sem("dve_passed")
        block = ctx.enter_context(nc.Block())

        def staggered(eng, front, back, lead=1):
            for g in range(lead):
                front(g, g % 2)

            def body(pair, last):
                for u in range(2):
                    if not (last and u + lead >= 2):
                        front(2 * pair + u + lead, (u + lead) % 2)
                    back(2 * pair + u, u)

            in_pairs(eng, body)

        def rows_count(g, u):
            return 16 * (g + 2 - u)

        def first_col(c):
            return P + sum(n for _, n in LATER[:c])

        @block.sync
        def _(sp):
            same = sp.value_load(same_rows[0:1, 0:1], min_val=0, max_val=1)
            with sp.If(same == 1):
                for dst, src in ((ident[:], d["consts"][:, const_cols("ident")]), (masks[:], d["chunk_masks"]),
                                 (delta_rows[:], d["delta"].rearrange("(b t) -> b t", b=SEQS)),
                                 (a_bc[:], d["A_log"][0, 0].partition_broadcast(P)),
                                 (a_col[:], d["A_row"].rearrange("(n a) -> n a", a=1))):
                    sp.dma_start(dst, src).then_inc(loaded, 16)

                def load(g, u, nth):
                    sp.wait_ge(row_parts_ready, PARTS * (g - 1) if nth > 1 else 0)
                    sp.dma_start(bc_rows[:, u], d["xp_T"][g, 0:2 * N]).then_inc(rows_loaded[u], 16)
                    sp.dma_start(c_rows[:, u], d["xp_T"][g, N:2 * N]).then_inc(rows_loaded[u], 16)

                def body(pair, last):
                    for u in range(2):
                        load(2 * pair + u, u, 1 if isinstance(pair, int) and pair == 0 else 2)

                in_pairs(sp, body)

        @block.gpsimd
        def _(pool):
            same = pool.value_load(same_rows[0:1, 0:1], min_val=0, max_val=1)
            with pool.If(same == 1):
                def front(g, u):
                    pool.wait_ge(c_turned_ready, g + 1)
                    b = seg_bc[:, u, 1, :, 0:N].unsqueeze(3).to_broadcast([P, GS, N, C])
                    nc.gpsimd.tensor_tensor(c_turned[:, u], c_turned[:, u], b, ALU.mult).then_inc(bc_ready, 1)
                    if not (isinstance(g, int) and g < 2):
                        pool.wait_ge(off_done, g - 1)
                    pool.wait_ge(rows_loaded[u], rows_count(g, u))
                    pool.wait_ge(row_decay_ready, GS * (g + 1))
                    seqs = bc_rows[0:N, u].rearrange("n (s t) -> n s t", s=GS)
                    nc.gpsimd.tensor_tensor(row_parts[:, u, :, 0:P], row_decay[:, u, :, 0:P], seqs,
                                            ALU.mult).then_inc(row_parts_ready, 1)
                    seqs = c_rows[:, u].rearrange("n (s t) -> n s t", s=GS)
                    for c, n in LATER:
                        cols = slice(first_col(c), first_col(c) + n)
                        nc.gpsimd.tensor_tensor(row_parts[:, u, :, cols], row_decay[:, u, :, cols],
                                                seqs[:, :, (c + 1) * C:], ALU.mult).then_inc(row_parts_ready, 1)

                staggered(pool, front, lambda g, u: None)

        @block.scalar
        def _(act):
            same = act.value_load(same_rows[0:1, 0:1], min_val=0, max_val=1)
            with act.If(same == 1):
                act.wait_ge(loaded, 5 * 16)
                for a in (a_bc, a_col):
                    nc.scalar.activation(a[:], a[:], ACT.Exp).then_inc(a_ready, 1)
                act.wait_ge(a_ready, 2)
                for a in (a_bc, a_col):
                    nc.scalar.activation(a[:], a[:], ACT.Copy, scale=-1.0).then_inc(a_ready, 1)
                act.wait_ge(a_ready, 4)

                def copy_seg(g, u):
                    act.wait_ge(seg_done, g + 1)
                    if not (isinstance(g, int) and g < 2):
                        act.wait_ge(inside_ready, g - 1)
                    nc.scalar.activation(seg_bc[:, u], ps_seg[:, u, 0:2 * GS * C].rearrange(
                        "p (w s t) -> p w s t", w=2, s=GS), ACT.Copy).then_inc(seg_ready, 1)
                    if not (isinstance(g, int) and g < 2):
                        act.wait_ge(row_parts_ready, PARTS * (g - 1))

                def decay_rows(g, u, s):
                    act.wait_ge(rows_done, GS * g + s + 1)
                    nc.scalar.activation(row_decay[:, u, s], ps_rows[0:N, s % 2, 0:SEG_COLS], ACT.Exp,
                                         scale=a_col[:, 0:1]).then_inc(row_decay_ready, 1)

                def decay_inside(g, u, s):
                    act.wait_ge(seg_ready, g + 1)
                    for n in range(s * N // GS, (s + 1) * N // GS):
                        nc.scalar.activation(decay[:, u, :, n], seg_bc[:, u, 0], ACT.Exp,
                                             scale=a_bc[:, n:n + 1]).then_inc(decay_ready, 1)

                copy_seg(0, 0)
                for s in range(GS):
                    decay_rows(0, 0, s)

                def body(pair, last):
                    for u in range(2):
                        g = 2 * pair + u
                        ahead = not (last and u)
                        if ahead:
                            copy_seg(g + 1, 1 - u)
                        if not (isinstance(pair, int) and pair == 0):
                            act.wait_ge(inside_ready, g - 1)
                        for s in range(GS):
                            if ahead:
                                decay_rows(g + 1, 1 - u, s)
                            decay_inside(g, u, s)

                in_pairs(act, body)

        @block.vector
        def _(dve):
            same = dve.value_load(same_rows[0:1, 0:1], min_val=0, max_val=1)
            with dve.If(same == 1):
                nc.vector.memset(products[:], 0.0).then_inc(cleared, 1)
                dve.wait_ge(loaded, 5 * 16)
                dve.wait_ge(delta_turned, 1)
                nc.vector.tensor_copy(delta_T[:], ps_delta[:, 0:SEQS]).then_inc(delta_ready, 1)
                dve.wait_ge(delta_ready, 1)
                dve.wait_ge(cleared, 1)

                def steps(g, u):
                    here = delta_T[:, bass.ds(g * GS, GS)]
                    if not (isinstance(g, int) and g < 2):
                        dve.wait_ge(rows_done, GS * (g - 1))
                        dve.sem_inc(dve_passed, 1)
                    nc.vector.tensor_tensor(step_masks[:, u], masks[:, 0:P].unsqueeze(1).to_broadcast([P, GS, P]),
                                            here.unsqueeze(2).to_broadcast([P, GS, P]), ALU.mult).then_inc(steps_ready, 1)
                    nc.vector.tensor_copy(step_wide[:, u], here.unsqueeze(2).to_broadcast([P, GS, N])
                                          ).then_inc(steps_ready, 1)

                def front(g, u):
                    dve.wait_ge(seg_ready, g + 1)
                    src = seg_bc[:, u, 1, :, N:2 * N].unsqueeze(3).to_broadcast([P, GS, N, C])
                    nc.vector.transpose(c_turned[:, u], src).then_inc(c_turned_ready, 1)

                def back(g, u):
                    dve.wait_ge(off_done, g + 1)
                    dve.sem_inc(dve_passed, 1)
                    cuts = ps_off[:, u, 0:GS * (P - C)].rearrange("p (s t) -> p s t", s=GS)
                    for c, n in LATER:
                        rows = slice(c * C, (c + 1) * C)
                        nc.vector.tensor_copy(products[rows, bass.ds(g * GS, GS), (c + 1) * C:],
                                              cuts[rows, :, c * C:]).then_inc(off_ready, 1)
                    dve.wait_ge(bc_ready, g + 1)
                    dve.wait_ge(decay_ready, N * (g + 1))
                    flat = "p s n t -> p (s n t)"
                    nc.vector.tensor_tensor(decay[:, u].rearrange(flat), decay[:, u].rearrange(flat),
                                            c_turned[:, u].rearrange(flat), ALU.mult).then_inc(weighted, 1)
                    dve.wait_ge(weighted, g + 1)
                    nc.vector.tensor_reduce(inside[:], decay[:, u].rearrange("p s n t -> p s t n"), AX.X,
                                            ALU.add).then_inc(inside_ready, 1)
                    dve.wait_ge(inside_ready, g + 1)
                    for c in range(SEQ_LEN // C):
                        rows = slice(c * C, (c + 1) * C)
                        causal = masks[rows, SEG_COLS:].unsqueeze(1).to_broadcast([C, GS, C])
                        nc.vector.tensor_tensor(products[rows, bass.ds(g * GS, GS), c * C:(c + 1) * C],
                                                inside[rows], causal, ALU.mult)

                steps(0, 0)
                steps(1, 1)
                front(0, 0)

                def body(pair, last):
                    for u in range(2):
                        g = 2 * pair + u
                        if not last:
                            steps(g + 2, u)
                        if not (last and u):
                            front(g + 1, 1 - u)
                        back(g, u)

                in_pairs(dve, body)

        @block.tensor
        def _(pe):
            same = pe.value_load(same_rows[0:1, 0:1], min_val=0, max_val=1)
            with pe.If(same == 1):
                pe.wait_ge(loaded, 5 * 16)
                nc.tensor.transpose(ps_delta[:, 0:SEQS], delta_rows[:], ident[0:SEQS, 0:SEQS]).then_inc(delta_turned, 1)

                def front(g, u):
                    pe.wait_ge(rows_loaded[u], rows_count(g, u))
                    pe.wait_ge(steps_ready, 2 * (g + 1))
                    if not (isinstance(g, int) and g < 2):
                        pe.wait_ge(seg_ready, g - 1)
                    for s in range(GS):
                        nc.tensor.matmul(ps_seg[:, u, s * C:(s + 1) * C], step_masks[:, u, s], masks[:, SEG_COLS:],
                                         start=True, stop=True)
                    for s in range(GS):
                        op = nc.tensor.transpose(ps_seg[:, u, (GS + s) * C:(GS + s + 1) * C],
                                                 bc_rows[:, u, s * P:(s + 1) * P], ident[0:2 * N, 0:2 * N])
                    op.then_inc(seg_done, 1)
                    for s in range(GS):
                        pe.wait_ge(row_decay_ready, GS * g + s - 1 if s >= 2 else GS * g)
                        nc.tensor.matmul(ps_rows[0:N, s % 2, 0:SEG_COLS], step_wide[:, u, s], masks[:, 0:SEG_COLS],
                                         start=True, stop=True).then_inc(rows_done, 1)

                def back(g, u):
                    pe.wait_ge(row_parts_ready, PARTS * (g + 1))
                    if not (isinstance(g, int) and g < 2):
                        pe.wait_ge(off_ready, len(LATER) * (g - 1))
                    pe.sem_inc(pe_passed, 1)
                    for s in range(GS):
                        for c, n in LATER:
                            at = s * (P - C) + c * C
                            op = nc.tensor.matmul(ps_off[c * C:(c + 1) * C, u, at:at + n],
                                                  row_parts[:, u, s, c * C:(c + 1) * C],
                                                  row_parts[:, u, s, first_col(c):first_col(c) + n],
                                                  start=True, stop=True, skip_group_check=True)
                    op.then_inc(off_done, 1)

                staggered(pe, front, back)


def chunk_scan(nc, d, same_rows, products):
    with ExitStack() as ctx:
        sb, ps, sem = allocators(nc, ctx, "chunk_scan")
        w_out = sb("w_out", [P, KI, D_MODEL], F32)
        ident = sb("ident", [P, P], F32)
        d_skip = sb("d_skip", [P, KI], F32)
        delta_rows = sb("delta_rows", [SEQS, SEQ_LEN], F32)
        delta_T = sb("delta_T", [P, SEQS], F32)
        neg_half = sb("neg_half", [P, GS], F32)
        xc_T = sb("xc_T", [P, 2, KI, GT], F32)
        gate_T = sb("gate_T", [P, 2, KI, GT], F32)
        x_rows = sb("x_rows", [P, 2, GS, D_MODEL], F32)
        dx = sb("dx", [P, 2, GS, D_INNER], F32)
        y_T = sb("y_T", [P, 2, KI, GT], F32)
        sum_rows = sb("sum_rows", [P, GS, D_MODEL], F32)
        x1 = sb("x1", [P, 2, GS, D_MODEL], F32)
        stats = sb("stats", [P, GS, 6], F32)
        mean_var = sb("mean_var", [P, GS, 2], F32)
        rstd = sb("rstd", [P, GS], F32)
        ps_x = ps("ps_x", [P, 2, D_INNER], F32)
        ps_y = ps("ps_y", [P, 2, GT], F32)
        ps_out = ps("ps_out", [P, GS, D_MODEL], F32)
        ps_delta = ps("ps_delta", [P, 512], F32)
        loaded = sem("loaded")
        const_ready = sem("const_ready")
        delta_turned = sem("delta_turned")
        delta_ready = sem("delta_ready")
        xc_loaded = [sem(f"xc_loaded_{u}") for u in range(2)]
        gate_loaded = [sem(f"gate_loaded_{u}") for u in range(2)]
        x_loaded = [sem(f"x_loaded_{u}") for u in range(2)]
        x_turned = sem("x_turned")
        dx_ready = sem("dx_ready")
        y_done = sem("y_done")
        skip_added = sem("skip_added")
        y_ready = sem("y_ready")
        out_done = sem("out_done")
        sum_ready = sem("sum_ready")
        stats_ready = sem("stats_ready")
        mean_ready = sem("mean_ready")
        var_eps_ready = sem("var_eps_ready")
        rstd_ready = sem("rstd_ready")
        x1_ready = sem("x1_ready")
        x1_stored = [sem(f"x1_stored_{u}") for u in range(2)]
        dve_passed = sem("dve_passed")
        pool_passed = sem("pool_passed")
        block = ctx.enter_context(nc.Block())

        def in_steps(eng, turn, apply, finish):
            def body(pair, last):
                for u in range(2):
                    g = 2 * pair + u
                    if not (last and u):
                        turn(g + 1, 1 - u, pair + u + 1)
                    apply(g, u, pair + 1)
                    if u or not (isinstance(pair, int) and pair == 0):
                        finish(g - 1, 1 - u, pair + u)

            turn(0, 0, 1)
            in_pairs(eng, body)
            finish(GROUPS - 1, 1, PAIRS)

        def skip(g, u, nth):
            pass

        @block.sync
        def _(sp):
            same = sp.value_load(same_rows[0:1, 0:1], min_val=0, max_val=1)
            with sp.If(same == 1):
                for stored in x1_stored:
                    sp.sem_inc(stored, 16)

                def load(g, u):
                    sp.dma_start(xc_T[:, u], d["xc_T"][g]).then_inc(xc_loaded[u], 16)
                    sp.dma_start(gate_T[:, u], d["gate_T"][g]).then_inc(gate_loaded[u], 16)

                def load_x(g, u):
                    sp.dma_start(x_rows[:, u], d["x"][g]).then_inc(x_loaded[u], 16)

                for dst, src in ((ident[:], d["consts"][:, const_cols("ident")]), (d_skip[:], d["D_skip"]),
                                 (delta_rows[:], d["delta"].rearrange("(b t) -> b t", b=SEQS)), (w_out[:], d["W_out"])):
                    sp.dma_start(dst, src).then_inc(loaded, 16)
                for g in range(2):
                    load(g, g)
                    load_x(g, g)

                def store(g, u):
                    sp.wait_ge(x1_ready, GS * (g + 1))
                    sp.dma_start(d["x1"][g], x1[:, u]).then_inc(x1_stored[u], 16)

                def body(pair, last):
                    for u in range(2):
                        g = 2 * pair + u
                        if not last:
                            sp.wait_ge(y_ready, KI * (g + 1))
                            load(g + 2, u)
                        if u or not (isinstance(pair, int) and pair == 0):
                            if not (last and u):
                                sp.wait_ge(sum_ready, 2 * g)
                                load_x(g + 1, 1 - u)
                        if not (isinstance(pair, int) and pair == 0):
                            store(g - 2, u)

                in_pairs(sp, body)
                for u in range(2):
                    store(GROUPS - 2 + u, u)
                for stored in x1_stored:
                    sp.wait_ge(stored, 16 * (PAIRS + 1))

        @block.gpsimd
        def _(pool):
            same = pool.value_load(same_rows[0:1, 0:1], min_val=0, max_val=1)
            with pool.If(same == 1):
                nc.gpsimd.memset(neg_half[:], -0.5).then_inc(const_ready, 1)
                pool.wait_ge(const_ready, 1)

                def apply(g, u, nth):
                    pool.wait_ge(gate_loaded[u], 16 * nth)
                    for j in range(KI):
                        pool.wait_ge(skip_added, KI * g + j + 1)
                        nc.gpsimd.tensor_tensor(y_T[:, u, j], y_T[:, u, j], gate_T[:, u, j],
                                                ALU.mult).then_inc(y_ready, 1)

                def finish(g, u, nth):
                    pool.wait_ge(mean_ready, GS * (g + 1))
                    pool.sem_inc(pool_passed, 1)
                    nc.gpsimd.tensor_scalar(rstd[:], mean_var[:, :, 1], LN_EPS, None,
                                            ALU.add).then_inc(var_eps_ready, 1)
                    pool.wait_ge(var_eps_ready, g + 1)
                    nc.gpsimd.tensor_tensor(rstd[:], rstd[:], neg_half[:], ALU.pow).then_inc(rstd_ready, 1)

                in_steps(pool, skip, apply, finish)

        @block.scalar
        def _(act):
            same = act.value_load(same_rows[0:1, 0:1], min_val=0, max_val=1)
            with act.If(same == 1):
                act.wait_ge(delta_ready, 1)

                def turn(g, u, nth):
                    if not (isinstance(g, int) and g < 2):
                        act.wait_ge(y_done, KI * (g - 1))
                    for s in range(GS):
                        act.wait_ge(x_turned, GS * g + s + 1)
                        nc.scalar.activation(dx[:, u, s], ps_x[:, s % 2], ACT.Copy,
                                             scale=delta_T[:, bass.ds(g * GS + s, 1)]).then_inc(dx_ready, 1)

                in_steps(act, turn, skip, skip)

        @block.vector
        def _(dve):
            same = dve.value_load(same_rows[0:1, 0:1], min_val=0, max_val=1)
            with dve.If(same == 1):
                dve.wait_ge(loaded, 64)
                dve.wait_ge(delta_turned, 1)
                nc.vector.tensor_copy(delta_T[:], ps_delta[:, 0:SEQS]).then_inc(delta_ready, 1)

                def apply(g, u, nth):
                    dve.wait_ge(xc_loaded[u], 16 * nth)
                    if not (isinstance(g, int) and g < 2):
                        dve.wait_ge(out_done, g - 1)
                    for j in range(KI):
                        dve.wait_ge(y_done, KI * g + j + 1)
                        nc.vector.scalar_tensor_tensor(y_T[:, u, j], xc_T[:, u, j], d_skip[:, j:j + 1], ps_y[:, j % 2],
                                                       ALU.mult, ALU.add).then_inc(skip_added, 1)

                def normalise(g, u, nth):
                    dve.wait_ge(rstd_ready, g + 1)
                    dve.wait_ge(mean_ready, GS * (g + 1))
                    dve.wait_ge(x1_stored[u], 16 * nth)
                    for s in range(GS):
                        nc.vector.tensor_scalar(x1[:, u, s], sum_rows[:, s], mean_var[:, s, 0:1], rstd[:, s:s + 1],
                                                ALU.subtract, ALU.mult).then_inc(x1_ready, 1)

                def finish(g, u, nth):
                    if not (isinstance(g, int) and g == 0):
                        normalise(g - 1, 1 - u, nth - 1 + u)
                    dve.wait_ge(x1_ready, GS * g)
                    dve.wait_ge(out_done, g + 1)
                    dve.wait_ge(x_loaded[u], 16 * nth)
                    for s in range(0, GS, 2):
                        nc.vector.scalar_tensor_tensor(sum_rows[:, s:s + 2], x_rows[:, u, s:s + 2], 2.0,
                                                       ps_out[:, s:s + 2], ALU.mult, ALU.add).then_inc(sum_ready, 1)
                    for s in range(GS):
                        dve.wait_ge(sum_ready, 2 * g + s // 2 + 1)
                        nc.vector.bn_stats(stats[:, s], sum_rows[:, s]).then_inc(stats_ready, 1)
                    dve.wait_ge(stats_ready, GS * (g + 1))
                    dve.sem_inc(dve_passed, 1)
                    for s in range(GS):
                        nc.vector.bn_aggr(mean_var[:, s], stats[:, s]).then_inc(mean_ready, 1)

                in_steps(dve, skip, apply, finish)
                normalise(GROUPS - 1, 1, PAIRS)

        @block.tensor
        def _(pe):
            same = pe.value_load(same_rows[0:1, 0:1], min_val=0, max_val=1)
            with pe.If(same == 1):
                pe.wait_ge(loaded, 64)
                nc.tensor.transpose(ps_delta[:, 0:SEQS], delta_rows[:], ident[0:SEQS, 0:SEQS]).then_inc(delta_turned, 1)

                def turn(g, u, nth):
                    pe.wait_ge(xc_loaded[u], 16 * nth)
                    for s in range(GS):
                        pe.wait_ge(dx_ready, GS * g + s - 1 if s >= 2 else GS * g)
                        for j in range(KI):
                            op = nc.tensor.transpose(ps_x[:, s % 2, j * P:(j + 1) * P],
                                                     xc_T[:, u, j, s * P:(s + 1) * P], ident[:])
                        op.then_inc(x_turned, 1)

                def apply(g, u, nth):
                    pe.wait_ge(dx_ready, GS * (g + 1))
                    for j in range(KI):
                        pe.wait_ge(skip_added, KI * g + j - 1 if j >= 2 else KI * g)
                        for s in range(GS):
                            op = nc.tensor.matmul(ps_y[:, j % 2, s * P:(s + 1) * P], dx[:, u, s, j * P:(j + 1) * P],
                                                  products[:, bass.ds(g * GS + s, 1)], start=True, stop=True)
                        op.then_inc(y_done, 1)

                def finish(g, u, nth):
                    pe.wait_ge(sum_ready, 2 * g)
                    pe.wait_ge(y_ready, KI * (g + 1))
                    for s in range(GS):
                        for j in range(KI):
                            op = nc.tensor.matmul(ps_out[:, s], y_T[:, u, j, s * P:(s + 1) * P], w_out[:, j],
                                                  start=(j == 0), stop=(j == KI - 1))
                    op.then_inc(out_done, 1)

                in_steps(pe, turn, apply, finish)


def retention(nc, d, logits):
    with ExitStack() as ctx:
        sb, ps, sem = allocators(nc, ctx, "retention")
        ident = sb("ident", [P, P], F32)
        w_q = sb("w_q", [P, KM, D_MODEL], F32)
        w_k = sb("w_k", [P, KM, D_MODEL], F32)
        w_v = sb("w_v", [P, KM, D_MODEL], F32)
        router = sb("router", [P, KM, EXPERTS], F32)
        router_bias = sb("router_bias", [P, GS, EXPERTS], F32)
        w_gate = sb("w_gate", [P, KM, D_FF], F32)
        w_up = sb("w_up", [P, KM, D_FF], F32)
        w_down = sb("w_down", [P, KF, D_MODEL], F32)
        raw_weights = (w_q, w_k, w_v, router, w_gate, w_up)
        w_q, w_k, w_v, router, w_gate, w_up = split_weights = [
            sb(f"{n}_parts", [P, 2, *w.shape[1:]], F32R)
            for n, w in zip(("w_q", "w_k", "w_v", "router", "w_gate", "w_up"), raw_weights)]
        tables = {n: sb(n, [P, GS, P], F32) for n in ("q_cos", "q_sin", "k_cos", "k_sin", "decay")}
        neg_half = sb("neg_half", [P, GS], F32)
        x1 = sb("x1", [P, 2, GS, D_MODEL], F32)
        c_rows = sb("c_rows", [P, 2, GS, D_MODEL], F32)
        x1_T = sb("x1_T", [P, 2, KM, GT], F32R)
        c_T = sb("c_T", [P, 2, KM, GT], F32R)
        parts = sb("parts", [P, 2, 4, GT], F32)
        turned_qk = sb("turned_qk", [P, 2, 2, GT], F32)
        v = sb("v", [P, GS, D_MODEL], F32)
        scores_T = sb("scores_T", [P, GT], F32)
        sum_rows = sb("sum_rows", [P, GS, D_MODEL], F32)
        x2 = sb("x2", [P, 2, GS, D_MODEL], F32)
        x2_T = sb("x2_T", [P, 2, KM, GT], F32R)
        silu_T = sb("silu_T", [P, 2, GT], F32)
        h_T = sb("h_T", [P, KF, GT], F32)
        base = sb("base", [P, GS, D_MODEL], F32)
        stats = sb("stats", [P, GS, 6], F32)
        mean_var = sb("mean_var", [P, GS, 2], F32)
        rstd = sb("rstd", [P, GS], F32)
        zeros = sb("zeros", [P, ZERO_TILES * D_MODEL], F32)
        ps_turn = ps("ps_turn", [P, KM, GT], F32)
        ps_wide = ps("ps_wide", [P, 3, GT], F32)
        ps_rows = ps("ps_rows", [P, GS, D_MODEL], F32)
        ps_small = ps("ps_small", [P, GT], F32)
        weights_loaded = sem("weights_loaded")
        rows_loaded = [sem(f"rows_loaded_{u}") for u in range(2)]
        const_ready = sem("const_ready")
        x1_turned = sem("x1_turned")
        x1_T_ready = sem("x1_T_ready")
        c_turned = sem("c_turned")
        c_T_ready = sem("c_T_ready")
        list_zeroed = sem("list_zeroed")
        x2_turned = sem("x2_turned")
        x2_T_ready = sem("x2_T_ready")
        w_high_ready = sem("w_high_ready")
        w_ready = sem("w_ready")
        high_ready = sem("high_ready")
        q_done = sem("q_done")
        k_done = sem("k_done")
        v_done = sem("v_done")
        v_ready = sem("v_ready")
        parts_ready = sem("parts_ready")
        xpos_ready = sem("xpos_ready")
        scores_done = sem("scores_done")
        decayed = sem("decayed")
        attended = sem("attended")
        sum_ready = sem("sum_ready")
        stats_ready = sem("stats_ready")
        mean_ready = sem("mean_ready")
        var_eps_ready = sem("var_eps_ready")
        rstd_ready = sem("rstd_ready")
        x2_ready = sem("x2_ready")
        logits_done = sem("logits_done")
        logits_ready = sem("logits_ready")
        gate_done = sem("gate_done")
        up_done = sem("up_done")
        silu_ready = sem("silu_ready")
        h_ready = sem("h_ready")
        down_done = sem("down_done")
        base_ready = sem("base_ready")
        x2_stored = [sem(f"x2_stored_{u}") for u in range(2)]
        base_stored = sem("base_stored")
        dve_passed = sem("dve_passed")
        pool_passed = sem("pool_passed")
        block = ctx.enter_context(nc.Block())
        WEIGHTS = 16 * (9 + 5 * GS + GS - 1)

        def in_steps(eng, step):
            step((0, 0), None)

            def body(pair, last):
                for u in range(2):
                    g = 2 * pair + u
                    step(None if last and u else (g + 1, 1 - u), (g, u))

            in_pairs(eng, body)

        @block.sync
        def _(sp):
            for stored in x2_stored:
                sp.sem_inc(stored, 16)

            def load(g, u):
                sp.dma_start(x1[:, u], d["x1"][g]).then_inc(rows_loaded[u], 16)
                sp.dma_start(c_rows[:, u], d["ctx"][g]).then_inc(rows_loaded[u], 16)

            sp.dma_start(ident[:], d["consts"][:, const_cols("ident")]).then_inc(weights_loaded, 16)
            load(0, 0)
            for dst, name in zip((*raw_weights, w_down),
                                 ("W_q", "W_k", "W_v", "router", "shared_gate", "shared_up", "shared_down")):
                sp.dma_start(dst[:], d[name]).then_inc(weights_loaded, 16)
            for s in range(GS):
                for name, table in tables.items():
                    sp.dma_start(table[:, s], d["consts"][:, const_cols(name)]).then_inc(weights_loaded, 16)
                sp.dma_start(router_bias[:, s], d["router_bias"].partition_broadcast(P)).then_inc(weights_loaded, 16)
            load(1, 1)

            def body(pair, last):
                for u in range(2):
                    g = 2 * pair + u
                    if not last:
                        sp.wait_ge(sum_ready, 2 * (g + 1))
                        load(g + 2, u)
                    sp.wait_ge(x2_ready, GS * (g + 1))
                    sp.dma_start(d["x2"][g], x2[:, u]).then_inc(x2_stored[u], 16)
                    sp.wait_ge(base_ready, 2 * (g + 1))
                    sp.dma_start(d["base"][g], base[:]).then_inc(base_stored, 16)

            in_pairs(sp, body)
            for stored in x2_stored:
                sp.wait_ge(stored, 16 * (PAIRS + 1))
            sp.wait_ge(base_stored, 16 * GROUPS)

        @block.gpsimd
        def _(pool):
            nc.gpsimd.memset(neg_half[:], -0.5).then_inc(const_ready, 1)
            pool.wait_ge(const_ready, 2)

            def step(attention, expert):
                if not attention:
                    return
                g, u = attention
                pool.wait_ge(scores_done, g)
                for which in range(2):
                    pool.wait_ge(parts_ready, 8 * g + 4 * which + 4)
                    for half, op in enumerate((ALU.subtract, ALU.add)):
                        nc.gpsimd.tensor_tensor(turned_qk[:, which, half], parts[:, which, 2 * half],
                                                parts[:, which, 2 * half + 1], op).then_inc(xpos_ready, 1)
                pool.wait_ge(mean_ready, GS * (g + 1))
                pool.sem_inc(pool_passed, 1)
                nc.gpsimd.tensor_scalar(rstd[:], mean_var[:, :, 1], LN_EPS, None, ALU.add).then_inc(var_eps_ready, 1)
                pool.wait_ge(var_eps_ready, g + 1)
                nc.gpsimd.tensor_tensor(rstd[:], rstd[:], neg_half[:], ALU.pow).then_inc(rstd_ready, 1)

            in_steps(pool, step)

        @block.scalar
        def _(act):
            act.wait_ge(const_ready, 2)
            act.wait_ge(weights_loaded, WEIGHTS)
            for m in range(ZERO_PARTS):
                act.dma_start(d["sorted_parts"][m], zeros[:]).then_inc(list_zeroed, 16)

            for raw, parts_of in zip(raw_weights, split_weights):
                nc.scalar.activation(parts_of[:, 0], raw[:], ACT.Copy).then_inc(w_high_ready, 1)

            def round_off(turned, dst, g):
                for k in range(KM):
                    act.wait_ge(turned, KM * g + k + 1)
                    nc.scalar.activation(dst[:, 0, k], ps_turn[:, k], ACT.Copy).then_inc(high_ready, 1)

            def step(attention, expert):
                if attention:
                    g, _ = attention
                    round_off(x1_turned, x1_T, g)
                    round_off(c_turned, c_T, g)
                    act.wait_ge(v_done, g + 1)
                    nc.scalar.activation(v[:], ps_rows[:], ACT.Copy).then_inc(v_ready, 1)
                if expert:
                    g, _ = expert
                    round_off(x2_turned, x2_T, g)
                    for i in range(KF):
                        act.wait_ge(gate_done, KF * g + i + 1)
                        if i:
                            act.wait_ge(h_ready, KF * g + i - 1)
                        nc.scalar.activation(silu_T[:, i % 2], ps_wide[:, 2 * i % 3], ACT.Silu).then_inc(silu_ready, 1)

            in_steps(act, step)
            act.wait_ge(list_zeroed, 16 * ZERO_PARTS)

        @block.vector
        def _(dve):
            nc.vector.memset(zeros[:], 0.0).then_inc(const_ready, 1)
            dve.wait_ge(weights_loaded, WEIGHTS)

            def by_seq(row):
                return row.rearrange("p (s t) -> p s t", s=GS)

            for i, (raw, parts_of) in enumerate(zip(raw_weights, split_weights)):
                dve.wait_ge(w_high_ready, i + 1)
                nc.vector.tensor_tensor(parts_of[:, 1], raw[:], parts_of[:, 0].bitcast(F32),
                                        ALU.subtract).then_inc(w_ready, 1)

            def rest(dst, before, ready):
                for k in range(KM):
                    dve.wait_ge(high_ready, before + k + 1)
                    nc.vector.tensor_tensor(dst[:, 1, k], ps_turn[:, k], dst[:, 0, k].bitcast(F32),
                                            ALU.subtract).then_inc(ready, 1)

            def xpos_parts(g, which):
                done, cos, sin = ((q_done, "q_cos", "q_sin"), (k_done, "k_cos", "k_sin"))[which]
                dve.wait_ge(xpos_ready, 4 * g)
                dve.wait_ge(done, g + 1)
                for i, (half, table) in enumerate(((0, cos), (1, sin), (1, cos), (0, sin))):
                    nc.vector.tensor_tensor(by_seq(parts[:, which, i]), by_seq(ps_wide[:, half]),
                                            tables[table][:], ALU.mult).then_inc(parts_ready, 1)

            def decay_scores(g):
                dve.wait_ge(scores_done, g + 1)
                dve.wait_ge(attended, g)
                nc.vector.tensor_tensor(by_seq(scores_T[:]), by_seq(ps_small[:]), tables["decay"][:],
                                        ALU.mult).then_inc(decayed, 1)

            def sum_and_stats(g, u):
                dve.wait_ge(rows_loaded[u], 16 * (g + 2 - u))
                dve.wait_ge(attended, g + 1)
                for s in range(0, GS, 2):
                    nc.vector.tensor_tensor(sum_rows[:, s:s + 2], x1[:, u, s:s + 2], ps_rows[:, s:s + 2],
                                            ALU.add).then_inc(sum_ready, 1)
                for s in range(GS):
                    dve.wait_ge(sum_ready, 2 * g + s // 2 + 1)
                    nc.vector.bn_stats(stats[:, s], sum_rows[:, s]).then_inc(stats_ready, 1)
                dve.wait_ge(stats_ready, GS * (g + 1))
                dve.sem_inc(dve_passed, 1)
                for s in range(GS):
                    nc.vector.bn_aggr(mean_var[:, s], stats[:, s]).then_inc(mean_ready, 1)

            def normalize(g, u):
                dve.wait_ge(rstd_ready, g + 1)
                dve.wait_ge(mean_ready, GS * (g + 1))
                dve.wait_ge(x2_stored[u], 8 * (g + 2 - u))
                for s in range(GS):
                    nc.vector.tensor_scalar(x2[:, u, s], sum_rows[:, s], mean_var[:, s, 0:1], rstd[:, s:s + 1],
                                            ALU.subtract, ALU.mult).then_inc(x2_ready, 1)

            def add_bias(g):
                dve.wait_ge(logits_done, g + 1)
                nc.vector.tensor_tensor(logits[:, bass.ds(g * GS, GS), :],
                                        ps_small[:, 0:GS * EXPERTS].rearrange("p (s e) -> p s e", s=GS),
                                        router_bias[:], ALU.add).then_inc(logits_ready, 1)
                dve.wait_ge(down_done, g)

            def hidden(g, i):
                dve.wait_ge(up_done, KF * g + i + 1)
                dve.wait_ge(silu_ready, KF * g + i + 1)
                nc.vector.tensor_tensor(h_T[:, i], silu_T[:, i % 2], ps_wide[:, (2 * i + 1) % 3],
                                        ALU.mult).then_inc(h_ready, 1)

            def expert_out(g, u):
                dve.wait_ge(down_done, g + 1)
                dve.wait_ge(base_stored, 16 * g)
                for s in range(0, GS, 2):
                    nc.vector.tensor_tensor(base[:, s:s + 2], x2[:, u, s:s + 2], ps_rows[:, s:s + 2],
                                            ALU.add).then_inc(base_ready, 1)

            def step(attention, expert):
                if attention:
                    g = attention[0]
                    before = KM * (3 * g - 1) if expert else 0
                    rest(x1_T, before, x1_T_ready)
                    rest(c_T, before + KM, c_T_ready)
                    xpos_parts(g, 0)
                if expert:
                    rest(x2_T, KM * (3 * expert[0] + (4 if attention else 2)), x2_T_ready)
                if attention:
                    xpos_parts(attention[0], 1)
                if expert:
                    add_bias(expert[0])
                    hidden(expert[0], 0)
                if attention:
                    decay_scores(attention[0])
                if expert:
                    hidden(expert[0], 1)
                if attention:
                    sum_and_stats(*attention)
                if expert:
                    for i in range(2, KF):
                        hidden(expert[0], i)
                if attention:
                    normalize(*attention)
                if expert:
                    expert_out(*expert)

            in_steps(dve, step)

        @block.tensor
        def _(pe):
            pe.wait_ge(weights_loaded, WEIGHTS)
            pe.wait_ge(w_ready, len(raw_weights))

            def seq(s):
                return slice(s * P, (s + 1) * P)

            def turn(rows, done, read, reads):
                for k in range(KM):
                    if reads is not None:
                        pe.wait_ge(read, reads + k)
                    for s in range(GS):
                        op = nc.tensor.transpose(ps_turn[:, k, seq(s)], rows[:, s, k * P:(k + 1) * P], ident[:])
                    op.then_inc(done, 1)

            def query_and_value(g, u):
                started = isinstance(g, int) and g < 2
                pe.wait_ge(rows_loaded[u], 16 * (g + 2 - u))
                turn(x1[:, u], x1_turned, x2_T_ready, None if started else KM * (g - 2) + 1)
                turn(c_rows[:, u], c_turned, x1_T_ready, KM * g + 1)
                if not started:
                    pe.wait_ge(h_ready, KF * (g - 1))
                pe.wait_ge(x1_T_ready, KM * (g + 1))
                project(w_q, x1_T, q_done)
                if started:
                    pe.wait_ge(sum_ready, 2 * g)
                else:
                    pe.wait_ge(base_ready, 2 * (g - 1))
                pe.wait_ge(c_T_ready, KM * (g + 1))
                for s in range(GS):
                    for n, (c_part, w_part, k) in enumerate(PASSES):
                        op = nc.tensor.matmul(ps_rows[:, s], c_T[:, c_part, k, seq(s)], w_v[:, w_part, k],
                                              start=(n == 0), stop=(n == len(PASSES) - 1))
                op.then_inc(v_done, 1)

            def key(g):
                pe.wait_ge(parts_ready, 8 * g + 4)
                project(w_k, c_T, k_done)

            def project(w, src, done):
                for half in range(2):
                    for n, (w_part, src_part, k) in enumerate(PASSES):
                        op = nc.tensor.matmul(ps_wide[:, half], w[:, w_part, k, half * P:(half + 1) * P],
                                              src[:, src_part, k], start=(n == 0), stop=(n == len(PASSES) - 1))
                op.then_inc(done, 1)

            def score(g):
                pe.wait_ge(logits_ready, g)
                pe.wait_ge(xpos_ready, 4 * (g + 1))
                for s in range(GS):
                    for half in range(2):
                        op = nc.tensor.matmul(ps_small[:, seq(s)], turned_qk[:, 1, half, seq(s)],
                                              turned_qk[:, 0, half, seq(s)], start=(half == 0), stop=(half == 1))
                op.then_inc(scores_done, 1)

            def attend(g):
                pe.wait_ge(v_ready, g + 1)
                pe.wait_ge(decayed, g + 1)
                for s in range(GS):
                    op = nc.tensor.matmul(ps_rows[:, s], scores_T[:, seq(s)], v[:, s], start=True, stop=True)
                op.then_inc(attended, 1)

            def turn_x2(g, u, ahead):
                pe.wait_ge(x2_ready, GS * (g + 1))
                turn(x2[:, u], x2_turned, c_T_ready, KM * (g + ahead) + 1)

            def route(g, ahead):
                pe.wait_ge(x2_T_ready, KM * (g + 1))
                pe.wait_ge(decayed, g + 1)
                for s in range(GS):
                    for n, (x_part, w_part, k) in enumerate(PASSES):
                        op = nc.tensor.matmul(ps_small[:, s * EXPERTS:(s + 1) * EXPERTS], x2_T[:, x_part, k, seq(s)],
                                              router[:, w_part, k], start=(n == 0), stop=(n == len(PASSES) - 1))
                op.then_inc(logits_done, 1)
                pe.wait_ge(parts_ready, 8 * (g + 1 + ahead))

            def gate_up(g, i):
                if i >= 2:
                    pe.wait_ge(h_ready, KF * g + i - 1)
                for n, (w_part, x_part, k) in enumerate(PASSES):
                    op = nc.tensor.matmul(ps_wide[:, 2 * i % 3], w_gate[:, w_part, k, seq(i)], x2_T[:, x_part, k],
                                          start=(n == 0), stop=(n == len(PASSES) - 1))
                op.then_inc(gate_done, 1)
                if i >= 1:
                    pe.wait_ge(silu_ready, KF * g + i)
                for n, (w_part, x_part, k) in enumerate(PASSES):
                    op = nc.tensor.matmul(ps_wide[:, (2 * i + 1) % 3], w_up[:, w_part, k, seq(i)], x2_T[:, x_part, k],
                                          start=(n == 0), stop=(n == len(PASSES) - 1))
                op.then_inc(up_done, 1)

            def down(g, ahead):
                pe.wait_ge(h_ready, KF * (g + 1))
                pe.wait_ge(sum_ready, 2 * (g + 1 + ahead))
                for s in range(GS):
                    for i in range(KF):
                        op = nc.tensor.matmul(ps_rows[:, s], h_T[:, i, seq(s)], w_down[:, i], start=(i == 0),
                                              stop=(i == KF - 1))
                op.then_inc(down_done, 1)

            def step(attention, expert):
                ahead = 1 if attention else 0
                if attention:
                    query_and_value(*attention)
                if expert:
                    turn_x2(*expert, ahead)
                if attention:
                    key(attention[0])
                if expert:
                    route(expert[0], ahead)
                    gate_up(expert[0], 0)
                if attention:
                    score(attention[0])
                if expert:
                    gate_up(expert[0], 1)
                if attention:
                    attend(attention[0])
                if expert:
                    for i in range(2, KF):
                        gate_up(expert[0], i)
                    down(expert[0], ahead)

            in_steps(pe, step)


def routing(nc, d, logits, slot, weight, tile_expert):
    with ExitStack() as ctx:
        sb, ps, sem = allocators(nc, ctx, "routing")
        B, E = SEQS, EXPERTS
        before = sb("before", [P, P], F32)
        ones = sb("ones", [P, P], F32)
        probs = sb("probs", [P, B, E], F32)
        key = sb("key", [P, B, E], F32)
        fill = sb("fill", [P, E, B], F32)
        tile_no = sb("tile_no", [P, SLOT_TILES, E], F32)
        best = sb("best", [P, 2, B], F32)
        hot = sb("hot", [P, 2, B, E], F32)
        scratch = sb("scratch", [P, B, E], F32)
        first = sb("first", [P, B], F32)
        chosen = sb("chosen", [P, B, E], F32)
        total = sb("total", [P, E, B], F32)
        running = sb("running", [P, E, B], F32)
        tiles = sb("tiles", [P, E], F32)
        tiles_end = sb("tiles_end", [P, E], F32)
        start = sb("start", [P, E], F32)
        place = sb("place", [P, B, E], F32)
        picked = sb("picked", [P, 2, B], F32)
        owner = sb("owner", [P, SLOT_TILES], F32)
        ps_rank = ps("ps_rank", [P, B, E], F32)
        ps_total = ps("ps_total", [P, B, E], F32)
        const_loaded = sem("const_loaded")
        probs_ready = sem("probs_ready")
        step = sem("step")
        counted = sem("counted")
        block = ctx.enter_context(nc.Block())
        CHOSEN = 1 + 13

        @block.sync
        def _(sp):
            sp.dma_start(before[:], d["consts"][:, const_cols("before")]).then_inc(const_loaded, 16)
            done = 0
            for dst, flat in ((key, "p b e -> p (b e)"), (fill, "p e b -> p (e b)"), (tile_no, "p i e -> p (i e)")):
                n = dst.shape[1] * dst.shape[2]
                sp.dma_start(dst[:].rearrange(flat), d["routing_tables"][done:done + n].partition_broadcast(P)
                             ).then_inc(const_loaded, 16)
                done += n
            sp.wait_ge(const_loaded, 4 * 16)

        @block.scalar
        def _(act):
            nc.scalar.activation(probs[:], logits[:], ACT.Sigmoid).then_inc(probs_ready, 1)

        @block.vector
        def _(dve):
            done = 0

            def then(op):
                nonlocal done
                op.then_inc(step, 1)
                done += 1
                dve.wait_ge(step, done)

            def over_e(a):
                return a.unsqueeze(2).to_broadcast([P, B, E])

            dve.wait_ge(const_loaded, 4 * 16)
            then(nc.vector.memset(ones[:], 1.0))
            dve.wait_ge(probs_ready, 1)
            for c in range(TOP_K):
                then(nc.vector.tensor_reduce(best[:, c], probs[:], AX.X, ALU.max))
                then(nc.vector.tensor_tensor(scratch[:], probs[:], over_e(best[:, c]), ALU.is_equal))
                then(nc.vector.tensor_tensor(scratch[:], scratch[:], key[:], ALU.mult))
                then(nc.vector.tensor_reduce(first[:], scratch[:], AX.X, ALU.max))
                then(nc.vector.tensor_tensor(hot[:, c], key[:], over_e(first[:]), ALU.is_equal))
                if c == 0:
                    then(nc.vector.scalar_tensor_tensor(probs[:], hot[:, 0], -2.0, probs[:], ALU.mult, ALU.add))
            then(nc.vector.tensor_tensor(first[:], best[:, 0], best[:, 1], ALU.add))
            then(nc.vector.tensor_tensor(chosen[:], hot[:, 0], hot[:, 1], ALU.add))
            assert done == CHOSEN
            then(nc.vector.reciprocal(first[:], first[:]))
            for c in range(TOP_K):
                then(nc.vector.tensor_tensor(weight[:, c], best[:, c], first[:], ALU.mult))
            dve.wait_ge(counted, 2)
            then(nc.vector.tensor_copy(total[:], ps_total[:].rearrange("p b e -> p e b")))
            for e in range(E):
                then(nc.vector.tensor_tensor_scan(running[:, e], ones[:, 0:B], total[:, e], 0.0, ALU.mult, ALU.add))
            then(nc.vector.tensor_tensor(fill[:], fill[:], running[:, :, B - 1:B].to_broadcast([P, E, B]), ALU.is_lt))
            then(nc.vector.tensor_reduce(tiles[:], fill[:], AX.X, ALU.add))
            then(nc.vector.tensor_tensor_scan(tiles_end[:], ones[:, 0:E], tiles[:], 0.0, ALU.mult, ALU.add))
            then(nc.vector.tensor_tensor(start[:], tiles_end[:], tiles[:], ALU.subtract))
            then(nc.vector.tensor_scalar(start[:], start[:], float(P), None, ALU.mult))
            then(nc.vector.tensor_tensor(running[:], running[:], total[:], ALU.subtract))
            then(nc.vector.tensor_tensor(place[:], ps_rank[:], running[:].rearrange("p e b -> p b e"), ALU.add))
            then(nc.vector.tensor_tensor(place[:], place[:], start[:].unsqueeze(1).to_broadcast([P, B, E]), ALU.add))
            for c in range(TOP_K):
                then(nc.vector.tensor_tensor(scratch[:], place[:], hot[:, c], ALU.mult))
                then(nc.vector.tensor_reduce(picked[:, c], scratch[:], AX.X, ALU.add))
            then(nc.vector.tensor_copy(slot[:], picked[:]))
            then(nc.vector.tensor_tensor(tile_no[:], tile_no[:], tiles_end[:].unsqueeze(1).to_broadcast(
                [P, SLOT_TILES, E]), ALU.is_ge))
            then(nc.vector.tensor_reduce(owner[:], tile_no[:], AX.X, ALU.add))
            then(nc.vector.tensor_scalar(owner[:], owner[:], float(E - 1), None, ALU.min))
            then(nc.vector.tensor_copy(tile_expert[:], owner[0:1, :]))

        @block.tensor
        def _(pe):
            pe.wait_ge(const_loaded, 4 * 16)
            pe.wait_ge(step, CHOSEN)
            flat = chosen[:].rearrange("p b e -> p (b e)")
            nc.tensor.matmul(ps_rank[:].rearrange("p b e -> p (b e)"), before[:], flat, start=True,
                             stop=True).then_inc(counted, 1)
            nc.tensor.matmul(ps_total[:].rearrange("p b e -> p (b e)"), ones[:], flat, start=True,
                             stop=True).then_inc(counted, 1)


def scatter(nc, d, slot, w_gate, w_up, w_down):
    RAW = 4
    CHUNKS = [(w, name, e) for w, name in ((w_gate, "gate_w"), (w_up, "up_w")) for e in range(EXPERTS)]
    with ExitStack() as ctx:
        sb, ps, sem = allocators(nc, ctx, "scatter")
        x2 = sb("x2", [P, 2, GS, D_MODEL], F32)
        places = sb("places", [P, 2, TOP_K, GS], U32)
        loaded = [sem(f"loaded_{u}") for u in range(2)]
        placed = sem("placed")
        pool_passed = sem("pool_passed")
        scattered = [sem(f"scattered_{u}") for u in range(2)]
        raw = sb("raw", [P, RAW, KM, D_FF], F32)
        raw_loaded = [sem(f"raw_loaded_{b}") for b in range(RAW)]
        high_ready = sem("high_ready")
        low_ready = sem("low_ready")
        down_loaded = sem("down_loaded")
        block = ctx.enter_context(nc.Block())

        @block.sync
        def _(sp):
            def body(pair, last):
                for u in range(2):
                    g = 2 * pair + u
                    sp.wait_ge(scattered[u], 16 * TOP_K * GS * pair)
                    sp.dma_start(x2[:, u], d["x2"][g]).then_inc(loaded[u], 16)

            in_pairs(sp, body)

        @block.scalar
        def _(act):
            def load(i):
                _, name, e = CHUNKS[i]
                act.dma_start(raw[:, i % RAW], d[name][e]).then_inc(raw_loaded[i % RAW], 16)

            for i in range(RAW):
                load(i)
            for e in range(EXPERTS):
                act.dma_start(w_down[:, e], d["down_w"][e]).then_inc(down_loaded, 16)
            for i, (w, _, e) in enumerate(CHUNKS):
                act.wait_ge(raw_loaded[i % RAW], 16 * (i // RAW + 1))
                nc.scalar.activation(w[:, 0, e], raw[:, i % RAW], ACT.Copy).then_inc(high_ready, 1)
                if 1 <= i <= len(CHUNKS) - RAW:
                    act.wait_ge(low_ready, i)
                    load(i - 1 + RAW)
            act.wait_ge(down_loaded, 16 * EXPERTS)

        @block.vector
        def _(dve):
            for i, (w, _, e) in enumerate(CHUNKS):
                dve.wait_ge(high_ready, i + 1)
                nc.vector.tensor_tensor(w[:, 1, e], raw[:, i % RAW], w[:, 0, e].bitcast(F32),
                                        ALU.subtract).then_inc(low_ready, 1)

        @block.gpsimd
        def _(pool):
            def body(pair, last):
                for u in range(2):
                    g = 2 * pair + u
                    pool.wait_ge(scattered[u], 16 * TOP_K * GS * pair)
                    nc.gpsimd.tensor_copy(places[:, u], slot[:, :, bass.ds(g * GS, GS)]).then_inc(placed, 1)
                    pool.wait_ge(placed, g + 1)
                    pool.wait_ge(loaded[u], 16 * (pair + 1))
                    pool.sem_inc(pool_passed, 1)
                    for s in range(GS):
                        for c in range(TOP_K):
                            pool.indirect_dma_start(
                                out=d["sorted"][:, :],
                                out_offset=bass.IndirectOffsetOnAxis(ap=places[:, u, c, s:s + 1], axis=0),
                                in_=x2[:, u, s], in_offset=None).then_inc(scattered[u], 16)

            in_pairs(pool, body)
            for done in scattered:
                pool.wait_ge(done, 16 * TOP_K * GS * PAIRS)


def experts(nc, d, tile_expert, w_gate, w_up, w_down):
    with ExitStack() as ctx:
        sb, ps, sem = allocators(nc, ctx, "experts")
        ident = sb("ident", [P, P], F32)
        x = sb("x", [P, 2, D_MODEL], F32)
        x_T = sb("x_T", [P, 2, 2, KM, P], F32R)
        silu = sb("silu", [P, 2, D_FF], F32)
        h = sb("h", [P, 2, D_FF], F32)
        h_T = sb("h_T", [P, KF, P], F32)
        y = sb("y", [P, 2, D_MODEL], F32)
        ps_turn = ps("ps_turn", [P, 2, 512], F32)
        ps_gate = ps("ps_gate", [P, 2, D_FF], F32)
        ps_up = ps("ps_up", [P, 2, D_FF], F32)
        ps_h_T = ps("ps_h_T", [P, KF, P], F32)
        ps_y = ps("ps_y", [P, 512], F32)
        const_loaded = sem("const_loaded")
        x_loaded = [sem(f"x_loaded_{u}") for u in range(2)]
        x_turned = sem("x_turned")
        x_high_ready = sem("x_high_ready")
        x_T_ready = sem("x_T_ready")
        gate_done = sem("gate_done")
        up_done = sem("up_done")
        silu_ready = sem("silu_ready")
        h_ready = sem("h_ready")
        h_turned = sem("h_turned")
        h_T_ready = sem("h_T_ready")
        y_done = sem("y_done")
        y_ready = sem("y_ready")
        y_stored = [sem(f"y_stored_{u}") for u in range(2)]
        block = ctx.enter_context(nc.Block())

        TILE_PAIRS = SLOT_TILES // 2

        def in_steps(eng, turn_x, up, turn_h, down):
            turn_x(0, 0)
            turn_x(1, 1)
            up(0, 0)

            def body(pair, last):
                for u in range(2):
                    i = 2 * pair + u
                    turn_h(i, u)
                    if not (last and u):
                        up(i + 1, 1 - u)
                    if not last:
                        turn_x(i + 2, u)
                    down(i, u)

            in_pairs(eng, body, TILE_PAIRS)

        def skip(i, u):
            pass

        def started(i):
            return isinstance(i, int) and i < 2

        @block.sync
        def _(sp):
            for u in range(2):
                sp.dma_start(x[:, u], d["sorted_tiles"][u]).then_inc(x_loaded[u], 16)
            sp.dma_start(ident[:], d["consts"][:, const_cols("ident")]).then_inc(const_loaded, 16)

            def load(i, u):
                sp.wait_ge(x_turned, i - 1)
                sp.dma_start(x[:, u], d["sorted_tiles"][i]).then_inc(x_loaded[u], 16)

            def store(i, u):
                sp.wait_ge(y_ready, i + 1)
                sp.dma_start(d["expert_tiles"][i], y[:, u]).then_inc(y_stored[u], 16)

            def body(pair, last):
                for u in range(2):
                    load(2 * pair + u + 4, u)
                    store(2 * pair + u, u)

            for u in range(2):
                load(u + 2, u)
            in_pairs(sp, body, TILE_PAIRS - 2)
            for i in range(SLOT_TILES - 4, SLOT_TILES):
                store(i, i % 2)
            for stored in y_stored:
                sp.wait_ge(stored, 16 * TILE_PAIRS)

        @block.scalar
        def _(act):
            def turn_x(i, u):
                act.wait_ge(x_turned, i + 1)
                nc.scalar.activation(x_T[:, u, 0], ps_turn[:, u, 0:D_MODEL].rearrange("p (k t) -> p k t", k=KM),
                                     ACT.Copy).then_inc(x_high_ready, 1)

            def up(i, u):
                act.wait_ge(gate_done, i + 1)
                nc.scalar.activation(silu[:, u], ps_gate[:, u], ACT.Silu).then_inc(silu_ready, 1)

            def turn_h(i, u):
                act.wait_ge(h_turned, i + 1)
                nc.scalar.activation(h_T[:], ps_h_T[:], ACT.Copy).then_inc(h_T_ready, 1)

            in_steps(act, turn_x, up, turn_h, skip)

        @block.vector
        def _(dve):
            def turn_x(i, u):
                dve.wait_ge(x_high_ready, i + 1)
                nc.vector.tensor_tensor(x_T[:, u, 1], ps_turn[:, u, 0:D_MODEL].rearrange("p (k t) -> p k t", k=KM),
                                        x_T[:, u, 0].bitcast(F32), ALU.subtract).then_inc(x_T_ready, 1)

            def up(i, u):
                dve.wait_ge(silu_ready, i + 1)
                dve.wait_ge(up_done, i + 1)
                nc.vector.tensor_tensor(h[:, u], silu[:, u], ps_up[:, u], ALU.mult).then_inc(h_ready, 1)

            def down(i, u):
                dve.wait_ge(y_done, i + 1)
                if not started(i):
                    dve.wait_ge(y_stored[u], 8 * (i - u))
                nc.vector.tensor_copy(y[:, u], ps_y[:, 0:D_MODEL]).then_inc(y_ready, 1)

            in_steps(dve, turn_x, up, skip, down)

        @block.tensor
        def _(pe):
            pe.wait_ge(const_loaded, 16)

            def turn_x(i, u):
                pe.wait_ge(x_loaded[u], 8 * (i - u + 2))
                if not started(i):
                    pe.wait_ge(x_T_ready, i - 1)
                for k in range(KM):
                    op = nc.tensor.transpose(ps_turn[:, u, k * P:(k + 1) * P], x[:, u, k * P:(k + 1) * P], ident[:])
                op.then_inc(x_turned, 1)

            def up(i, u):
                e = pe.value_load(tile_expert[0:1, bass.ds(i, 1)], min_val=0, max_val=EXPERTS - 1)
                if not started(i):
                    pe.wait_ge(h_ready, i - 1)
                pe.wait_ge(x_T_ready, i + 1)
                for w, out, done in ((w_gate, ps_gate, gate_done), (w_up, ps_up, up_done)):
                    for n, (x_part, w_part, k) in enumerate(PASSES):
                        op = nc.tensor.matmul(out[:, u], x_T[:, u, x_part, k], w[:, w_part, bass.ds(e, 1), k],
                                              start=(n == 0), stop=(n == len(PASSES) - 1))
                    op.then_inc(done, 1)

            def turn_h(i, u):
                pe.wait_ge(h_ready, i + 1)
                pe.wait_ge(h_T_ready, i)
                for k in range(KF):
                    op = nc.tensor.transpose(ps_h_T[:, k], h[:, u, k * P:(k + 1) * P], ident[:])
                op.then_inc(h_turned, 1)

            def down(i, u):
                e = pe.value_load(tile_expert[0:1, bass.ds(i, 1)], min_val=0, max_val=EXPERTS - 1)
                pe.wait_ge(h_T_ready, i + 1)
                pe.wait_ge(y_ready, i)
                for k in range(KF):
                    op = nc.tensor.matmul(ps_y[:, 0:D_MODEL], h_T[:, k], w_down[:, bass.ds(e, 1), k], start=(k == 0),
                                          stop=(k == KF - 1))
                op.then_inc(y_done, 1)

            in_steps(pe, turn_x, up, turn_h, down)


def combine(nc, d, slot, weight):
    with ExitStack() as ctx:
        sb, ps, sem = allocators(nc, ctx, "combine")
        neg_half = sb("neg_half", [P, GS], F32)
        base = sb("base", [P, 2, GS, D_MODEL], F32)
        rows = sb("rows", [P, 2, GS, TOP_K, D_MODEL], F32)
        places = sb("places", [P, 2, TOP_K, GS], U32)
        part = sb("part", [P, GS, D_MODEL], F32)
        total = sb("total", [P, GS, D_MODEL], F32)
        out = sb("out", [P, 2, GS, D_MODEL], F32)
        stats = sb("stats", [P, GS, 6], F32)
        mean_var = sb("mean_var", [P, GS, 2], F32)
        rstd = sb("rstd", [P, GS], F32)
        const_ready = sem("const_ready")
        base_loaded = [sem(f"base_loaded_{u}") for u in range(2)]
        gathered = [sem(f"gathered_{u}") for u in range(2)]
        placed = sem("placed")
        part_ready = sem("part_ready")
        total_ready = sem("total_ready")
        stats_ready = sem("stats_ready")
        mean_ready = sem("mean_ready")
        out_ready = sem("out_ready")
        out_stored = [sem(f"out_stored_{u}") for u in range(2)]
        var_eps_ready = sem("var_eps_ready")
        rstd_ready = sem("rstd_ready")
        dve_passed = sem("dve_passed")
        pool_passed = sem("pool_passed")
        block = ctx.enter_context(nc.Block())

        @block.sync
        def _(sp):
            for stored in out_stored:
                sp.sem_inc(stored, 16)
            sp.dma_start(base[:, 0], d["base"][0]).then_inc(base_loaded[0], 16)
            sp.dma_start(base[:, 1], d["base"][1]).then_inc(base_loaded[1], 16)

            def body(pair, last):
                for u in range(2):
                    g = 2 * pair + u
                    if not last:
                        sp.wait_ge(part_ready, GS * (g + 1))
                        sp.dma_start(base[:, u], d["base"][g + 2]).then_inc(base_loaded[u], 16)
                    sp.wait_ge(out_ready, GS * (g + 1))
                    sp.dma_start(d["out"][g], out[:, u]).then_inc(out_stored[u], 16)

            in_pairs(sp, body)
            for stored in out_stored:
                sp.wait_ge(stored, 16 * (PAIRS + 1))

        @block.gpsimd
        def _(pool):
            nc.gpsimd.memset(neg_half[:], -0.5).then_inc(const_ready, 1)
            pool.wait_ge(const_ready, 1)

            def gather(g, u):
                nc.gpsimd.tensor_copy(places[:, u], slot[:, :, bass.ds(g * GS, GS)]).then_inc(placed, 1)
                pool.wait_ge(placed, g + 1)
                pool.sem_inc(pool_passed, 1)
                for s in range(GS):
                    for c in range(TOP_K):
                        pool.indirect_dma_start(
                            out=rows[:, u, s, c], out_offset=None, in_=d["expert_rows"][:, :],
                            in_offset=bass.IndirectOffsetOnAxis(ap=places[:, u, c, s:s + 1], axis=0)
                        ).then_inc(gathered[u], 16)

            gather(0, 0)
            gather(1, 1)

            def body(pair, last):
                for u in range(2):
                    g = 2 * pair + u
                    pool.wait_ge(mean_ready, GS * (g + 1))
                    pool.sem_inc(pool_passed, 1)
                    nc.gpsimd.tensor_scalar(rstd[:], mean_var[:, :, 1], LN_EPS, None,
                                            ALU.add).then_inc(var_eps_ready, 1)
                    pool.wait_ge(var_eps_ready, g + 1)
                    nc.gpsimd.tensor_tensor(rstd[:], rstd[:], neg_half[:], ALU.pow).then_inc(rstd_ready, 1)
                    if not last:
                        pool.wait_ge(total_ready, GS * (g + 1))
                        gather(g + 2, u)

            in_pairs(pool, body)

        @block.vector
        def _(dve):
            def body(pair, last):
                for u in range(2):
                    g = 2 * pair + u
                    dve.wait_ge(base_loaded[u], 16 * (pair + 1))
                    dve.wait_ge(gathered[u], 16 * GS * TOP_K * (pair + 1))
                    for s in range(GS):
                        b = g * GS + s
                        nc.vector.scalar_tensor_tensor(part[:, s], rows[:, u, s, 0], weight[:, 0, bass.ds(b, 1)],
                                                       base[:, u, s], ALU.mult, ALU.add).then_inc(part_ready, 1)
                    for s in range(GS):
                        b = g * GS + s
                        dve.wait_ge(part_ready, GS * g + s + 1)
                        nc.vector.scalar_tensor_tensor(total[:, s], rows[:, u, s, 1], weight[:, 1, bass.ds(b, 1)],
                                                       part[:, s], ALU.mult, ALU.add).then_inc(total_ready, 1)
                    for s in range(GS):
                        dve.wait_ge(total_ready, GS * g + s + 1)
                        nc.vector.bn_stats(stats[:, s], total[:, s]).then_inc(stats_ready, 1)
                    dve.wait_ge(stats_ready, GS * (g + 1))
                    dve.sem_inc(dve_passed, 1)
                    for s in range(GS):
                        nc.vector.bn_aggr(mean_var[:, s], stats[:, s]).then_inc(mean_ready, 1)
                    dve.wait_ge(rstd_ready, g + 1)
                    dve.wait_ge(mean_ready, GS * (g + 1))
                    dve.wait_ge(out_stored[u], 16 * (pair + 1))
                    for s in range(GS):
                        nc.vector.tensor_scalar(out[:, u, s], total[:, s], mean_var[:, s, 0:1], rstd[:, s:s + 1],
                                                ALU.subtract, ALU.mult).then_inc(out_ready, 1)

            in_pairs(dve, body)


def launch_args(inputs):
    def chunks(a):
        return np.ascontiguousarray(a.reshape(a.shape[0] // P, P, -1).transpose(1, 0, 2))

    a = {n: np.asarray(v) for n, v in inputs.items()}
    halves = np.r_[0:D_MODEL:2, 1:D_MODEL:2]
    return {
        "x": a["x"], "ctx": a["ctx_1024"], "consts": shape_constants(),
        "chunk_masks": chunk_masks(), "routing_tables": routing_tables(), "A_row": a["L0_attn_A_log"][0],
        "W_in": chunks(a["L0_attn_W_in"]), "W_x": chunks(a["L0_attn_W_x"]), "W_out": chunks(a["L0_attn_W_out"]),
        "gamma": chunks(a["L0_attn_gamma"])[:, :, 0].copy(), "beta": chunks(a["L0_attn_beta"])[:, :, 0].copy(),
        "conv_wb": chunks(np.concatenate([a["L0_attn_conv_w"][:, 0], a["L0_attn_conv_b"][:, None]], axis=1)),
        "W_q": chunks(a["L0_xattn_Wq"][:, halves]), "W_k": chunks(a["L0_xattn_Wk"][:, halves]),
        "W_v": chunks(a["L0_xattn_Wv"]), "router": chunks(a["L0_ffn_router_w"].T), "router_bias": a["L0_ffn_routing_bias"],
        "shared_gate": chunks(a["L0_ffn_shared_gate"].T), "shared_up": chunks(a["L0_ffn_shared_up"].T),
        "shared_down": chunks(a["L0_ffn_shared_down"].T),
        **{n: np.stack([chunks(w) for w in a["L0_ffn_" + n]]) for n in ("gate_w", "up_w", "down_w")},
        "A_log": chunks(a["L0_attn_A_log"]), "D_skip": chunks(a["L0_attn_D_skip"])[:, :, 0].copy(),
    }



def views(t):
    d = dict(t)
    for name in ("x", "ctx", "out"):
        if name in t:
            d[name] = t[name].rearrange("(g s) t c -> g t s c", s=GS)
    if "xp" in t:
        d["xp_T"] = t["xp"].rearrange("c g t -> g c t")
        d["xp_rows"] = t["xp"]
        d["dt_row"] = t["xp"][2 * D_STATE].rearrange("g t -> (g t)")
        d["delta_groups"] = t["delta"].rearrange("(g t) -> g t", t=GT)
    if "sorted" in t:
        d["sorted_tiles"] = t["sorted"].rearrange("(i p) c -> i p c", p=P)
        d["sorted_parts"] = t["sorted"].rearrange("(m p r) c -> m p (r c)", m=ZERO_PARTS, p=P)
    if "expert_rows" in t:
        d["expert_tiles"] = t["expert_rows"].rearrange("(i p) c -> i p c", p=P)
    return d


SCRATCH = {"xc_T": [GROUPS, P, KI, GT], "gate_T": [GROUPS, P, KI, GT], "xp": [XP, GROUPS, GT],
           "delta": [TOKENS], "x1": [GROUPS, P, GS, D_MODEL], "x2": [GROUPS, P, GS, D_MODEL],
           "base": [GROUPS, P, GS, D_MODEL], "sorted": [SLOTS, D_MODEL], "expert_rows": [SLOTS, D_MODEL]}


def program(nc, t):
    t = dict(t)
    for name, shape in SCRATCH.items():
        t[name] = nc.dram_tensor(name, shape, F32).ap()
    d = views(t)
    mamba_in(nc, d)
    step_sizes(nc, d)
    with ExitStack() as ctx:
        sb, ps, sem = allocators(nc, ctx, "block")
        same_rows = sb("same_rows", [1, 1], I32)
        scan_choice(nc, d, same_rows)
        with ExitStack() as chunked:
            sb, ps, sem = allocators(nc, chunked, "block")
            products = sb("products", [P, SEQS, SEQ_LEN], F32)
            chunk_products(nc, d, same_rows, products)
            chunk_scan(nc, d, same_rows, products)
        mamba_scan(nc, d, same_rows)
    clear_semaphores(nc)
    with ExitStack() as ctx:
        sb, ps, sem = allocators(nc, ctx, "block")
        logits = sb("logits", [P, SEQS, EXPERTS], F32)
        slot = sb("slot", [P, TOP_K, SEQS], U32)
        weight = sb("weight", [P, TOP_K, SEQS], F32)
        tile_expert = sb("tile_expert", [1, SLOT_TILES], I32)
        retention(nc, d, logits)
        routing(nc, d, logits, slot, weight, tile_expert)
        with ExitStack() as weights:
            sb, ps, sem = allocators(nc, weights, "block")
            w_gate = sb("w_gate", [P, 2, EXPERTS, KM, D_FF], F32R)
            w_up = sb("w_up", [P, 2, EXPERTS, KM, D_FF], F32R)
            w_down = sb("w_down", [P, EXPERTS, KF, D_MODEL], F32)
            scatter(nc, d, slot, w_gate, w_up, w_down)
            experts(nc, d, tile_expert, w_gate, w_up, w_down)
        combine(nc, d, slot, weight)


def kernel(**inputs):
    import concourse.bacc as bacc
    from concourse.bass_utils import run_bass_kernel_spmd

    nc = bacc.Bacc("TRN2", target_bir_lowering=False, num_devices=1)
    arrays = launch_args(inputs)
    t = {n: nc.dram_tensor("in_" + n, a.shape, mybir.dt.from_np(a.dtype), kind="ExternalInput").ap()
         for n, a in arrays.items()}
    t["out"] = nc.dram_tensor("out_rows", [SEQS, SEQ_LEN, D_MODEL], F32, kind="ExternalOutput").ap()
    program(nc, t)
    r = run_bass_kernel_spmd(nc, [{"in_" + n: a for n, a in arrays.items()}], core_ids=[0])
    return r.results[0]["out_rows"]
```
